# Optimizing a Trainium2 kernel written in Bass

```python
import numpy as np
import jax
import jax.numpy as jnp

def _softmax(x, axis=-1):
    return jax.nn.softmax(x, axis=axis)

def _gelu(x):
    return jax.nn.gelu(x, approximate=True)

def _silu(x):
    return jax.nn.silu(x)

def _sigmoid(x):
    return jax.nn.sigmoid(x)

def _layernorm(x, axis=-1, eps=1e-05):
    m = jnp.mean(x, axis=axis, keepdims=True)
    v = jnp.var(x, axis=axis, keepdims=True)
    return (x - m) / jnp.sqrt(v + eps)

def _scatter_add(tgt, idx, src, axis=0):
    return tgt.at[idx].add(src)

def _segment_sum(src, seg, n):
    return jax.ops.segment_sum(src, seg, n)
kernel_name = 'mk_prb_d1_jaxref_r8_5b982f'

def setup_inputs(seed: int=0):
    np.random.seed(seed)
    _w = jnp.asarray

    def _L0_attn_setup():
        import jax, jax.numpy as jnp
        import numpy as np
        B, T, D = (2, 256, 512)
        H = 32
        HKV = 1
        HD = D // H
        key = jax.random.key(seed)
        ks = jax.random.split(key, 9)
        s = lambda fan_in: 1.0 / np.sqrt(fan_in)
        return {'x': jax.random.normal(ks[0], (B, T, D), dtype=jnp.float32), 'wq_w': jax.random.normal(ks[1], (H * HD, D), dtype=jnp.float32) * s(D), 'wq_b': jax.random.normal(ks[2], (H * HD,), dtype=jnp.float32) * 0.02, 'wk_w': jax.random.normal(ks[3], (HKV * HD, D), dtype=jnp.float32) * s(D), 'wk_b': jax.random.normal(ks[4], (HKV * HD,), dtype=jnp.float32) * 0.02, 'wv_w': jax.random.normal(ks[5], (HKV * HD, D), dtype=jnp.float32) * s(D), 'wv_b': jax.random.normal(ks[6], (HKV * HD,), dtype=jnp.float32) * 0.02, 'wo_w': jax.random.normal(ks[7], (D, H * HD), dtype=jnp.float32) * s(H * HD), 'wo_b': jax.random.normal(ks[8], (D,), dtype=jnp.float32) * 0.02}
    _L0_attn_in = _L0_attn_setup()

    def _L0_ffn_setup():
        import jax, jax.numpy as jnp
        import numpy as np
        _TRIPLES = [(1, 2, 3), (1, 4, 5), (1, 7, 6), (2, 4, 6), (2, 5, 7), (3, 4, 7), (3, 6, 5)]

        def _oct_struct():
            S = np.zeros((8, 8, 8), np.float32)
            S[0, 0, 0] = 1.0
            for i in range(1, 8):
                S[0, i, i] = 1.0
                S[i, 0, i] = 1.0
                S[i, i, 0] = -1.0
            for a, b, c in _TRIPLES:
                for x, y, z in ((a, b, c), (b, c, a), (c, a, b)):
                    S[x, y, z] = 1.0
                    S[y, x, z] = -1.0
            return jnp.asarray(S)
        S_OCT = _oct_struct()
        N_EMBD = 512
        HIDDEN = 1366

        def ternary_dequant(W):
            scale = jnp.mean(jnp.abs(W))
            Wq = scale * jnp.clip(jnp.round(W / scale), -1.0, 1.0)
            return W + jax.lax.stop_gradient(Wq - W)

        def oct_ternary_linear(xp, W):
            Wq = ternary_dequant(W)
            M = jnp.einsum('jik,jod->koid', S_OCT, Wq)
            return jnp.einsum('...id,koid->...ko', xp, M)
        key = jax.random.key(seed)
        k1, k2, k3, k4 = jax.random.split(key, 4)
        B, T = (2, 256)
        d8, h8 = (N_EMBD // 8, HIDDEN // 8)
        std_in = 1.0 / np.sqrt(N_EMBD)
        std_h = 1.0 / np.sqrt(HIDDEN)
        return {'x': jax.random.normal(k1, (B, T, N_EMBD), jnp.float32), 'w_gate': jax.random.normal(k2, (8, h8, d8), jnp.float32) * std_in, 'w_up': jax.random.normal(k3, (8, h8, d8), jnp.float32) * std_in, 'w_down': jax.random.normal(k4, (8, d8, h8), jnp.float32) * std_h}
    _L0_ffn_in = _L0_ffn_setup()
    _d = {'L0_attn_x': _L0_attn_in['x'], 'L0_attn_wq_w': _L0_attn_in['wq_w'], 'L0_attn_wq_b': _L0_attn_in['wq_b'], 'L0_attn_wk_w': _L0_attn_in['wk_w'], 'L0_attn_wk_b': _L0_attn_in['wk_b'], 'L0_attn_wv_w': _L0_attn_in['wv_w'], 'L0_attn_wv_b': _L0_attn_in['wv_b'], 'L0_attn_wo_w': _L0_attn_in['wo_w'], 'L0_attn_wo_b': _L0_attn_in['wo_b'], 'L0_ffn_w_gate': _L0_ffn_in['w_gate'], 'L0_ffn_w_up': _L0_ffn_in['w_up'], 'L0_ffn_w_down': _L0_ffn_in['w_down']}
    _x0 = _d['L0_attn_x']
    _d['L0_attn_x'] = jax.random.normal(jax.random.fold_in(jax.random.key(seed), 1), (2, 512, 512), dtype=_x0.dtype)
    del _x0
    return _d

def reference(L0_attn_x, L0_attn_wq_w, L0_attn_wq_b, L0_attn_wk_w, L0_attn_wk_b, L0_attn_wv_w, L0_attn_wv_b, L0_attn_wo_w, L0_attn_wo_b, L0_ffn_w_gate, L0_ffn_w_up, L0_ffn_w_down):

    def _L0_attn_ref(x, wq_w, wq_b, wk_w, wk_b, wv_w, wv_b, wo_w, wo_b):
        import jax, jax.numpy as jnp
        import numpy as np
        B, T, D = (2, 256, 512)
        H = 32
        HKV = 1
        HD = D // H
        b, t, d = x.shape
        q = (x @ wq_w.T + wq_b).reshape(b, t, H, HD)
        k = (x @ wk_w.T + wk_b).reshape(b, t, HKV, HD)
        v = (x @ wv_w.T + wv_b).reshape(b, t, HKV, HD)
        k1 = k[:, :, 0, :]
        v1 = v[:, :, 0, :]
        scores = jnp.einsum('bqhd,bkd->bhqk', q, k1) / jnp.sqrt(jnp.float32(HD))
        causal = jnp.tril(jnp.ones((t, t), dtype=bool))
        scores = jnp.where(causal, scores, -jnp.inf)
        weights = jax.nn.softmax(scores, axis=-1)
        attn = jnp.einsum('bhqk,bkd->bqhd', weights, v1)
        attn = attn.reshape(b, t, H * HD)
        return attn @ wo_w.T + wo_b

    def _L0_ffn_ref(x, w_gate, w_up, w_down):
        import jax, jax.numpy as jnp
        import numpy as np
        _TRIPLES = [(1, 2, 3), (1, 4, 5), (1, 7, 6), (2, 4, 6), (2, 5, 7), (3, 4, 7), (3, 6, 5)]

        def _oct_struct():
            S = np.zeros((8, 8, 8), np.float32)
            S[0, 0, 0] = 1.0
            for i in range(1, 8):
                S[0, i, i] = 1.0
                S[i, 0, i] = 1.0
                S[i, i, 0] = -1.0
            for a, b, c in _TRIPLES:
                for x, y, z in ((a, b, c), (b, c, a), (c, a, b)):
                    S[x, y, z] = 1.0
                    S[y, x, z] = -1.0
            return jnp.asarray(S)
        S_OCT = _oct_struct()
        N_EMBD = 512
        HIDDEN = 1366

        def ternary_dequant(W):
            scale = jnp.mean(jnp.abs(W))
            Wq = scale * jnp.clip(jnp.round(W / scale), -1.0, 1.0)
            return W + jax.lax.stop_gradient(Wq - W)

        def oct_ternary_linear(xp, W):
            Wq = ternary_dequant(W)
            M = jnp.einsum('jik,jod->koid', S_OCT, Wq)
            return jnp.einsum('...id,koid->...ko', xp, M)
        B, T, D = x.shape
        xp = x.reshape(B, T, 8, D // 8)
        gate = oct_ternary_linear(xp, w_gate).reshape(B, T, -1)
        up = oct_ternary_linear(xp, w_up).reshape(B, T, -1)
        h = jax.nn.silu(gate) * up
        hp = h.reshape(B, T, 8, h.shape[-1] // 8)
        out = oct_ternary_linear(hp, w_down).reshape(B, T, D)
        return out
    x = L0_attn_x
    xn = _layernorm(x, axis=-1)
    x = x + _L0_attn_ref(xn, L0_attn_wq_w, L0_attn_wq_b, L0_attn_wk_w, L0_attn_wk_b, L0_attn_wv_w, L0_attn_wv_b, L0_attn_wo_w, L0_attn_wo_b) + _L0_ffn_ref(xn, L0_ffn_w_gate, L0_ffn_w_up, L0_ffn_w_down)
    return x

_drawn_inputs = setup_inputs


def setup_inputs(seed=0):
    import zlib

    import numpy as np

    out = dict(_drawn_inputs(seed))
    spreads = {}
    factors = {'L0_attn_wq_b': 8.0, 'L0_attn_wk_b': 8.0, 'L0_attn_wv_b': 3.051, 'L0_attn_wo_b': 3.055}
    for name, (base, spread) in spreads.items():
        noise = np.random.default_rng([zlib.crc32(name.encode()), seed]).standard_normal(out[name].shape)
        drawn = base * np.exp(spread * noise) if base else spread * noise
        out[name] = jnp.asarray(drawn.astype(out[name].dtype))
    for name, factor in factors.items():
        out[name] = (out[name] * factor).astype(out[name].dtype)
    return out
```

```python
import numpy as np
import concourse.bass as bass
from concourse import mybir
from contextlib import ExitStack

FP32 = mybir.dt.float32
BF16 = mybir.dt.bfloat16
FP16 = mybir.dt.float16
ALU = mybir.AluOpType
ACT = mybir.ActivationFunctionType
AX = mybir.AxisListType

P = 128
B, T, D = 2, 512, 512
TOK = B * T
NT = TOK // P
TT = T // P
DC = D // P
H, HD = 32, 16
VW = HD + 1
J, OD, HID = 8, D // 8, 170
F = J * HID
MF = -(-F // P)
FL = F - (MF - 1) * P
GH = 4
NG = B * H // GH
GB = NG // B
GW = GH * T
PAIRS = [(0, 0), (0, 1), (0, 2), (1, 0), (1, 1), (2, 0)]
BANDS = len(PAIRS) * HD
ROWS = BANDS + 2
SLOTS = 4
BLOCKS = [(kc, t) for t in range(TT) for kc in range(t + 1)]
NBLK = len(BLOCKS)
UNITS = [(0, (0, 1, 2, 3), 4), (1, (0, 1, 2, 3), 2), (2, (0, 1), 1), (2, (2, 3), 1), (3, (0, 1), 1), (3, (2, 3), 1)]
NU = len(UNITS)
UNIT_AT = {0: 0, 1: 1, 3: 2, 5: 3, 7: 4, 9: 5}
SUMS_AT = [[(3, 0)], [(3, 1)], [(3, 2)], [(3, 3)], [(2, 0), (1, 0)], [(2, 1), (1, 1)], [(2, 2), (1, 2)],
           [(2, 3), (1, 3)], [(0, 0), (0, 1)], [(0, 2), (0, 3)]]
EPS = 1e-5
XS = 1024.0
HS = 0.125
MASKED = -1e30


def build(nc, x, wqT, wkT, wvT, woT, bq, bk, bv, bo, wg, wu, wd, signs, bands, out):
    ctx = ExitStack()
    with ctx:
        def sb(name, shape, dt=FP32):
            return ctx.enter_context(nc.sbuf_tensor(name, shape, dt))

        def sem(name):
            return ctx.enter_context(nc.semaphore(name))

        x_sb = sb("x_sb", [P, NT, D])
        xn = sb("xn", [P, 2, D])
        attnT = xn[:].rearrange("p s (c q) -> p s c q", c=DC)
        xnT = sb("xnT", [P, DC, TOK])
        mdT = xnT[:].rearrange("p c t -> p (c t)").bitcast(FP16)[:, 0:MF * D].rearrange("p (m n) -> p m n", m=MF)
        attn = xnT[:].rearrange("p c t -> p (c t)").rearrange("p (t n) -> p t n", t=NT)
        xhi = sb("xhi", [P, DC, TOK], FP16)
        xlo = sb("xlo", [P, DC, TOK], FP16)
        wq_sb = sb("wq_sb", [P, DC, D])
        wk_sb = sb("wk_sb", [P, DC, BANDS])
        wv_sb = sb("wv_sb", [P, DC, HD])
        wo_sb = sb("wo_sb", [P, DC, D])
        bq_sb = sb("bq_sb", [P, DC])
        bk_sb = sb("bk_sb", [BANDS, 1])
        bv_sb = sb("bv_sb", [P, HD])
        bo_sb = sb("bo_sb", [P, D])
        signs_sb = sb("signs_sb", [P, 2, DC, J])
        bands_sb = sb("bands_sb", [BANDS, 3])
        raw = sb("raw", [P, max(3 * F, SLOTS * GW // 2)])
        qstack = raw[0:ROWS, 0:SLOTS * GW // 2].bitcast(BF16)
        neg = sb("neg", [P, F], FP16)
        tern = sb("tern", [P, F], FP16)
        mg = sb("mg", [P, DC, F], FP16)
        mu = sb("mu", [P, DC, F], FP16)
        md = sb("md", [P, DC, F], FP16)
        hbuf = sb("hbuf", [P, 2, MF, TOK], FP16)
        probs = hbuf[:, :, 0:NBLK, :].bitcast(FP32)
        qpart = sb("qpart", [P, 3, 2, T], BF16)
        kpart = sb("kpart", [BANDS, 3, T], BF16)
        kband = sb("kband", [BANDS, 3, T], BF16)
        kstack = sb("kstack", [ROWS, TOK], BF16)
        v_sb = sb("v_sb", [P, NT, VW])
        sig = sb("sig", [P, 2, T])
        gated = sb("gated", [P, 2, T])
        hid = sb("hid", [P, 2, T])
        kf, kr = sig[0:BANDS, 0, :], sig[0:BANDS, 1, :]
        qf, qr = gated, hid
        stats = sb("stats", [P, NT, 6])
        mv = sb("mv", [P, NT, 2])
        vare = sb("vare", [P, NT])
        half = sb("half", [P, NT])
        rstd = sb("rstd", [P, NT])
        wsum = sb("wsum", [P, 3])
        scale = sb("scale", [P, 3])
        thr = sb("thr", [P, 3])
        nthr = sb("nthr", [P, 3])
        gscale = sb("gscale", [P, 1])
        fprod = sb("fprod", [P, 1])
        fscale = sb("fscale", [P, 1])
        ones = sb("ones", [P, P])
        identf = sb("identf", [P, P])
        ident16 = sb("ident16", [P, P], FP16)
        identb = sb("identb", [P, P], BF16)
        maskq = sb("maskq", [P, P], BF16)
        negm = sb("negm", [P, 2, GH, TT])
        mparts = sb("mparts", [P, 2, 2, GH * TT], BF16)
        mrows = sb("mrows", [2 * GH * TT, 2, P], BF16)
        rden = sb("rden", [P, TT, GH])
        ps = ctx.enter_context(nc.psum_tensor("ps", [P, 8, 512], FP32))
        q_dram = nc.dram_tensor("q_parts", [3, D, TOK], BF16, kind="Internal").ap()

        m_dram = nc.dram_tensor("minus_maxima", [NG, 2 * GH * TT, P], BF16, kind="Internal").ap()

        x_ld = [sem(f"x_ld{i}") for i in range(NT // 2)]
        wq_ld, wkv_ld, wo_ld, small_ld = sem("wq_ld"), sem("wkv_ld"), sem("wo_ld"), sem("small_ld")
        raw_ld = [sem(f"raw_ld{i}") for i in range(3)]
        filled, consts = sem("filled"), sem("consts")
        stats_done, mv_done, vare_ready, rstd_ready = sem("stats_done"), sem("mv_done"), sem("vare_ready"), sem("rstd_ready")
        xn_ready, xt_ready, xnT_ready, xhi_ready, xlo_ready = (sem("xn_ready"), sem("xt_ready"), sem("xnT_ready"),
                                                               sem("xhi_ready"), sem("xlo_ready"))
        xb_ready = sem("xb_ready")
        q_ready, q1_ready, qf_ready, qr_ready, q2_ready, q3_ready = (sem("q_ready"), sem("q1_ready"), sem("qf_ready"),
                                                                     sem("qr_ready"), sem("q2_ready"), sem("q3_ready"))
        q_out = [sem("q_out0"), sem("q_out1")]
        k_ready, kf_ready, kchain, v_ready, vsb_ready = (sem("k_ready"), sem("kf_ready"), sem("kchain"), sem("v_ready"),
                                                         sem("vsb_ready"))
        wsum_ready, total_ready, total_read, schain, scales_ready = (sem("wsum_ready"), sem("total_ready"), sem("total_read"),
                                                                     sem("schain"), sem("scales_ready"))
        neg_done, tern_done, built = sem("neg_done"), sem("tern_done"), sem("built")
        gate_ready, up_ready, sig_ready, gated_ready = sem("gate_ready"), sem("up_ready"), sem("sig_ready"), sem("gated_ready")
        hid_ready, hhi_ready, hlo_ready = sem("hid_ready"), sem("hhi_ready"), sem("hlo_ready")
        mdt_ready, mdT_ready, down_ready, down_used = sem("mdt_ready"), sem("mdT_ready"), sem("down_ready"), sem("down_used")
        stack_ld = [sem("stack_ld0"), sem("stack_ld1")]
        mrow_st = [sem("mrow_st0"), sem("mrow_st1")]
        mrow_ld = [sem("mrow_ld0"), sem("mrow_ld1")]
        rows_ready, rows_used, m1_ready, mparts_ready = sem("rows_ready"), sem("rows_used"), sem("m1_ready"), sem("mparts_ready")
        mt_ready, mt_read, cols_ready, exp_ready = sem("mt_ready"), sem("mt_read"), sem("cols_ready"), sem("exp_ready")
        cut_go = sem("cut_go")
        cut_ready, sums_ready, rden_ready, normed = sem("cut_ready"), sem("sums_ready"), sem("rden_ready"), sem("normed")
        at_ready, attnT_ready, o_ready, y_ready, y_out = (sem("at_ready"), sem("attnT_ready"), sem("o_ready"), sem("y_ready"),
                                                          sem("y_out"))

        block = ctx.enter_context(nc.Block())

        STEPS = [(-1, -1, "m"), (-1, 0, "mr"), (-1, 1, "mre"), (0, 0, "mres"), (0, 1, "mresw"), "loop", (6, 0, "mresw"), (6, 1, "resw"), (6, 2, "esw"), (6, 3, "sw")]
        LOOPED = (1, 6)

        def group(i, o):
            return 2 * i + o

        @block.sync
        def _(sp):
            x_t = x.rearrange("(n p) d -> p n d", p=P)
            for i in range(2):
                sp.dma_start(x_sb[:, 2 * i:2 * i + 2, :], x_t[:, 2 * i:2 * i + 2, :]).then_inc(x_ld[i], 16)
            sp.dma_start(wq_sb[:], wqT.rearrange("(c p) n -> p c n", p=P)).then_inc(wq_ld, 16)
            for i in range(2, 4):
                sp.dma_start(x_sb[:, 2 * i:2 * i + 2, :], x_t[:, 2 * i:2 * i + 2, :]).then_inc(x_ld[i], 16)
            for i, w in enumerate((wg, wu, wd)):
                sp.dma_start(raw[:, i * F:(i + 1) * F], w).then_inc(raw_ld[i], 16)
            sp.dma_start(wo_sb[:], woT.rearrange("(c p) n -> p c n", p=P)).then_inc(wo_ld, 16)
            for u in range(B * DC):
                b, m, s = u // DC, u % DC, u % 2
                sp.wait_ge(q1_ready, u + 1)
                sp.wait_ge(q2_ready, u + 1)
                sp.wait_ge(q3_ready, u + 1)
                sp.dma_start(q_dram[:, m * P:(m + 1) * P, b * T:(b + 1) * T].rearrange("r p t -> p r t"),
                             qpart[:, :, s, :]).then_inc(q_out[s], 16)

            def load_stack(i, o):
                g = group(i, o)
                for r, (part, _) in enumerate(PAIRS):
                    sp.dma_start(
                        qstack[r * HD:(r + 1) * HD, bass.ds((g % SLOTS) * GW, GW)].rearrange("d (h t) -> d h t", h=GH),
                        q_dram[part, bass.ds((g % GB) * GH * HD, GH * HD), bass.ds((g // GB) * T, T)]
                        .rearrange("(h d) t -> d h t", d=HD)).then_inc(stack_ld[o % 2], 16)

            def load_maxima(i, o):
                g = group(i, o)
                sp.wait_ge(mt_read, g + 1)
                sp.dma_start(m_dram[bass.ds(g, 1)].squeeze(0), mrows[:, o % 2, :]).then_inc(mrow_st[o % 2], 16)
                sp.wait_ge(mrow_st[o % 2], 16 * (i + o // 2 + 1))
                sp.dma_start(qstack[BANDS:ROWS, bass.ds((g % SLOTS) * GW, GW)],
                             m_dram[bass.ds(g, 1)].squeeze(0).rearrange("(r s) q -> r (s q)", r=2)).then_inc(mrow_ld[o % 2], 16)

            sp.wait_ge(q_out[0], 16 * B * DC // 2)
            sp.wait_ge(q_out[1], 16 * B * DC // 2)
            sp.wait_ge(tern_done, 3)
            load_stack(0, 0)
            load_stack(0, 1)
            sp.wait_ge(stack_ld[0], 16 * len(PAIRS))
            load_stack(0, 2)
            sp.wait_ge(stack_ld[1], 16 * len(PAIRS))
            load_stack(0, 3)

            def step(i, o, what, stack):
                if "r" in what:
                    load_maxima(i, o + 2)
                if stack:
                    sp.wait_ge(cols_ready, NBLK * (group(i, o) + 1))
                    load_stack(i, o + 4)

            for st in STEPS:
                if st == "loop":
                    with sp.Fori(*LOOPED) as i:
                        for o in range(2):
                            step(i, o, "mresw", True)
                else:
                    step(*st, st[0] == 0)

            out_t = out.rearrange("(n p) d -> p n d", p=P)
            for t in range(NT):
                sp.wait_ge(y_ready, t + 1)
                sp.dma_start(out_t[:, t, :], x_sb[:, t, :]).then_inc(y_out, 16)
            sp.wait_ge(y_out, 16 * NT)

        @block.gpsimd
        def _(pool):
            for m in (identf, ident16, identb, maskq):
                nc.gpsimd.memset(m[:], 0.0).then_inc(filled, 1)
            nc.gpsimd.memset(ones[:], 1.0).then_inc(filled, 1)
            nc.gpsimd.memset(half[:], -0.5).then_inc(filled, 1)
            nc.gpsimd.memset(v_sb[:, :, HD:VW], 1.0).then_inc(filled, 1)
            pool.wait_ge(filled, 7)
            nc.gpsimd.memset(kstack[BANDS:ROWS, :], 1.0).then_inc(filled, 1)
            pool.wait_ge(filled, 8)
            for m in (identf, ident16, identb):
                nc.gpsimd.affine_select(out=m[:], in_=m[:], compare_op=ALU.not_equal, fill=1.0, base=0,
                                        pattern=[[-1, P]], channel_multiplier=1).then_inc(consts, 1)
            nc.gpsimd.affine_select(out=maskq[:], in_=maskq[:], compare_op=ALU.is_ge, fill=MASKED, base=0,
                                    pattern=[[-1, P]], channel_multiplier=1).then_inc(consts, 1)

            def rsqrt(b):
                pool.wait_ge(vare_ready, b + 1)
                t = slice(b * TT, (b + 1) * TT)
                nc.gpsimd.tensor_tensor(rstd[:, t], vare[:, t], half[:, t], ALU.pow).then_inc(rstd_ready, 1)

            def q_rest(u):
                s = u % 2
                pool.wait_ge(qf_ready, u + 1)
                pool.wait_ge(q1_ready, u + 1)
                if u >= 2:
                    pool.wait_ge(q2_ready, u - 1)
                    pool.wait_ge(q3_ready, u - 1)
                nc.gpsimd.tensor_tensor(qr[:, s, :], qf[:, s, :], qpart[:, 0, s, :], ALU.subtract).then_inc(qr_ready, 1)

            def q_third(u):
                s = u % 2
                pool.wait_ge(qr_ready, u + 1)
                pool.wait_ge(q2_ready, u + 1)
                nc.gpsimd.tensor_tensor(qpart[:, 2, s, :], qr[:, s, :], qpart[:, 1, s, :], ALU.subtract).then_inc(q3_ready, 1)

            chain = [0]

            def link(ins):
                chain[0] += 1
                ins.then_inc(kchain, 1)
                pool.wait_ge(kchain, chain[0])

            def k_parts(b):
                pool.wait_ge(kf_ready, b + 1)
                link(nc.gpsimd.tensor_copy(kpart[:, 0, :], kf))
                link(nc.gpsimd.tensor_tensor(kr, kf, kpart[:, 0, :], ALU.subtract))
                link(nc.gpsimd.tensor_copy(kpart[:, 1, :], kr))
                link(nc.gpsimd.tensor_tensor(kpart[:, 2, :], kr, kpart[:, 1, :], ALU.subtract))
                for r in range(3):
                    link(nc.gpsimd.tensor_scalar(kband[:, r, :], kpart[:, r, :], bands_sb[:, r:r + 1], None, ALU.mult))
                link(nc.gpsimd.tensor_tensor(kband[:, 0, :], kband[:, 0, :], kband[:, 1, :], ALU.add))
                link(nc.gpsimd.tensor_tensor(kstack[0:BANDS, b * T:(b + 1) * T], kband[:, 0, :], kband[:, 2, :], ALU.add))

            rsqrt(0)
            rsqrt(1)
            pool.wait_ge(small_ld, 16 * 6)
            for b in range(B):
                for m in range(DC):
                    u = b * DC + m
                    q_rest(u)
                    if u:
                        q_third(u - 1)
                k_parts(b)
            q_third(B * DC - 1)
            pool.wait_ge(xn_ready, NT)
            nc.gpsimd.tensor_tensor(x_sb[:], x_sb[:], bo_sb[:].unsqueeze(1).to_broadcast([P, NT, D]),
                                    ALU.add).then_inc(xb_ready, 1)

            def hidden_low(m, b, rows):
                n = 2 * m + b
                pool.wait_ge(hid_ready, n + 1)
                pool.wait_ge(hhi_ready, n + 1)
                cols = slice(b * T, (b + 1) * T)
                nc.gpsimd.tensor_tensor(hbuf[0:rows, 1, bass.ds(m, 1), cols].squeeze(1), hid[0:rows, b, :],
                                        hbuf[0:rows, 0, bass.ds(m, 1), cols].squeeze(1), ALU.subtract).then_inc(hlo_ready, 1)

            with pool.Fori(0, MF - 1) as m:
                for b in range(B):
                    hidden_low(m, b, P)
            for b in range(B):
                hidden_low(MF - 1, b, FL)

            def step(i, o, what):
                if "e" not in what:
                    return
                e = group(i, o + 1)
                for s, (kc, t) in enumerate(BLOCKS):
                    if kc == t:
                        pool.wait_ge(exp_ready, NBLK * e + s + 1)
                        pool.sem_inc(cut_go, 1)
                        blk = probs[:, (o + 1) % 2, s, :]
                        nc.gpsimd.affine_select(out=blk, in_=blk, compare_op=ALU.is_ge, fill=0.0, base=0,
                                                pattern=[[0, GH], [1, P]], channel_multiplier=-1).then_inc(cut_ready, 1)

            for st in STEPS:
                if st == "loop":
                    with pool.Fori(*LOOPED) as i:
                        for o in range(2):
                            step(i, o, "mresw")
                else:
                    step(*st)

        @block.scalar
        def _(act):
            act.dma_start(wk_sb[:], wkT.rearrange("(c p) n -> p c n", p=P)).then_inc(wkv_ld, 16)
            act.dma_start(wv_sb[:], wvT.rearrange("(c p) n -> p c n", p=P)).then_inc(wkv_ld, 16)
            act.dma_start(bq_sb[:], bq).then_inc(small_ld, 16)
            act.dma_start(bk_sb[:], bk).then_inc(small_ld, 16)
            act.dma_start(bv_sb[:], bv.rearrange("(a n) -> a n", a=1).to_broadcast([P, HD])).then_inc(small_ld, 16)
            act.dma_start(bo_sb[:], bo.rearrange("(a n) -> a n", a=1).to_broadcast([P, D])).then_inc(small_ld, 16)
            act.dma_start(signs_sb[:].rearrange("p a c k -> p (a c k)"), signs).then_inc(small_ld, 16)
            act.dma_start(bands_sb[:], bands).then_inc(small_ld, 16)

            def q_first(u):
                s = u % 2
                act.wait_ge(q_ready, u + 1)
                if u >= 2:
                    act.wait_ge(q_out[s], 16 * (u // 2))
                nc.scalar.activation(qpart[:, 0, s, :], ps[:, 2 + u % DC, :], ACT.Identity,
                                     bias=bq_sb[:, u % DC:u % DC + 1]).then_inc(q1_ready, 1)

            def q_second(u):
                s = u % 2
                act.wait_ge(qr_ready, u + 1)
                nc.scalar.activation(qpart[:, 1, s, :], qr[:, s, :], ACT.Copy).then_inc(q2_ready, 1)

            for b in range(B):
                for n in range(b * TT, (b + 1) * TT):
                    act.wait_ge(xt_ready, n + 1)
                    src = ps[:, n % 2, :].rearrange("p (c q) -> p c q", c=DC)
                    nc.scalar.activation(xnT[:, :, n * P:(n + 1) * P], src, ACT.Copy).then_inc(xnT_ready, 1)
                    nc.scalar.activation(xhi[:, :, n * P:(n + 1) * P], src, ACT.Copy, scale=XS).then_inc(xhi_ready, 1)
                act.wait_ge(small_ld, 16 * 6)
                for m in range(DC):
                    u = b * DC + m
                    q_first(u)
                    if u:
                        q_second(u - 1)
                act.wait_ge(k_ready, b + 1)
                if b:
                    act.wait_ge(kchain, 9 * b)
                nc.scalar.activation(kf, ps[0:BANDS, 6, :], ACT.Identity, bias=bk_sb[:, 0:1]).then_inc(kf_ready, 1)
            q_second(B * DC - 1)
            act.wait_ge(kchain, 9 * B)
            act.wait_ge(scales_ready, 1)

            def hidden(m, b, rows):
                n = 2 * m + b
                cols = slice(b * T, (b + 1) * T)
                act.wait_ge(gate_ready, n + 1)
                nc.scalar.activation(sig[0:rows, b, :], ps[0:rows, 2 * b, :], ACT.Sigmoid,
                                     scale=gscale[0:rows, 0:1]).then_inc(sig_ready, 1)
                act.wait_ge(hid_ready, n + 1)
                nc.scalar.activation(hbuf[0:rows, 0, bass.ds(m, 1), cols].squeeze(1), hid[0:rows, b, :],
                                     ACT.Copy).then_inc(hhi_ready, 1)

            with act.Fori(0, MF - 1) as m:
                for b in range(B):
                    hidden(m, b, P)
            for b in range(B):
                hidden(MF - 1, b, FL)
            for m in range(MF):
                rows = P if m < MF - 1 else FL
                act.wait_ge(mdt_ready, m + 1)
                nc.scalar.activation(mdT[0:rows, m, :], ps[0:rows, 4 + m % 2, 0:D // 2].bitcast(FP16),
                                     ACT.Copy).then_inc(mdT_ready, 1)

            def step(i, o, what):
                if "e" not in what:
                    return
                e = group(i, o + 1)
                par = (o + 1) % 2
                for s in range(NBLK):
                    act.wait_ge(cols_ready, NBLK * e + s + 1)
                    if s == 0 and "w" in what:
                        act.wait_ge(sums_ready, e - 1)
                    nc.scalar.activation(probs[:, par, s, :], ps[:, 4 + s % 2, :], ACT.Exp,
                                         scale=float(HD) ** -0.5).then_inc(exp_ready, 1)

            for st in STEPS:
                if st == "loop":
                    with act.Fori(*LOOPED) as i:
                        for o in range(2):
                            step(i, o, "mresw")
                else:
                    step(*st)

            for t in range(NT):
                act.wait_ge(at_ready, t + 1)
                if t >= 2:
                    act.wait_ge(o_ready, t - 1)
                nc.scalar.activation(attnT[:, t % 2], ps[:, t % 2, :].rearrange("p (c q) -> p c q", c=DC),
                                     ACT.Copy).then_inc(attnT_ready, 1)

        @block.vector
        def _(dve):
            def statistics(b):
                for n in range(b * TT, (b + 1) * TT):
                    dve.wait_ge(x_ld[n // 2], 16)
                    nc.vector.bn_stats(stats[:, n, :], x_sb[:, n, :]).then_inc(stats_done, 1)
                for n in range(b * TT, (b + 1) * TT):
                    dve.wait_ge(stats_done, n + 1)
                    nc.vector.bn_aggr(mv[:, n, :], stats[:, n, :]).then_inc(mv_done, 1)
                dve.wait_ge(mv_done, (b + 1) * TT)
                t = slice(b * TT, (b + 1) * TT)
                nc.vector.tensor_scalar(vare[:, t], mv[:, t, 1], EPS, None, ALU.add).then_inc(vare_ready, 1)

            def normalise(b):
                dve.wait_ge(rstd_ready, b + 1)
                for n in range(b * TT, (b + 1) * TT):
                    if n >= 2:
                        dve.wait_ge(xt_ready, n - 1)
                    nc.vector.tensor_scalar(xn[:, n % 2, :], x_sb[:, n, :], mv[:, n, 0:1], rstd[:, n:n + 1],
                                            ALU.subtract, ALU.mult).then_inc(xn_ready, 1)

            def x_low(b):
                dve.wait_ge(xnT_ready, (b + 1) * TT)
                dve.wait_ge(xhi_ready, (b + 1) * TT)
                t = slice(b * T, (b + 1) * T)
                for c in range(DC):
                    last = nc.vector.scalar_tensor_tensor(out=xlo[:, c, t], in0=xnT[:, c, t], scalar=XS,
                                                          in1=xhi[:, c, t], op0=ALU.mult, op1=ALU.subtract)
                last.then_inc(xlo_ready, 1)

            def q_full(u):
                s = u % 2
                dve.wait_ge(q1_ready, u + 1)
                if u >= 2:
                    dve.wait_ge(qr_ready, u - 1)
                nc.vector.tensor_scalar(qf[:, s, :], ps[:, 2 + u % DC, :], bq_sb[:, u % DC:u % DC + 1], None,
                                        ALU.add).then_inc(qf_ready, 1)

            def v_full(b):
                dve.wait_ge(v_ready, b + 1)
                nc.vector.tensor_tensor(v_sb[:, b * TT:(b + 1) * TT, 0:HD],
                                        ps[:, 7, 0:TT * HD].rearrange("p (t d) -> p t d", t=TT),
                                        bv_sb[:].unsqueeze(1).to_broadcast([P, TT, HD]), ALU.add).then_inc(vsb_ready, 1)

            def expand(w, kind, dst):
                cols = slice(w * F, (w + 1) * F)
                if w:
                    dve.wait_ge(built, w)
                nc.vector.tensor_scalar(neg[:], raw[:, cols], nthr[:, w:w + 1], None, ALU.is_lt).then_inc(neg_done, 1)
                dve.wait_ge(neg_done, w + 1)
                nc.vector.scalar_tensor_tensor(out=tern[:], in0=raw[:, cols], scalar=thr[:, w:w + 1], in1=neg[:],
                                               op0=ALU.is_gt, op1=ALU.subtract).then_inc(tern_done, 1)
                dve.wait_ge(tern_done, w + 1)
                for c in range(DC):
                    for k in range(J):
                        j = (2 * c) ^ k
                        last = nc.vector.tensor_scalar(dst[:, c, k * HID:(k + 1) * HID], tern[:, j * HID:(j + 1) * HID],
                                                       signs_sb[:, kind, c, k:k + 1], None, ALU.mult)
                last.then_inc(built, 1)

            statistics(0)
            normalise(0)
            statistics(1)
            for w in range(3):
                dve.wait_ge(raw_ld[w], 16)
                nc.vector.tensor_reduce(wsum[:, w:w + 1], raw[:, w * F:(w + 1) * F], axis=AX.X, op=ALU.add,
                                        apply_absolute_value=True).then_inc(wsum_ready, 1)
            dve.wait_ge(small_ld, 16 * 6)
            for m in range(DC):
                q_full(m)
            v_full(0)
            dve.wait_ge(total_ready, 1)
            nc.vector.tensor_scalar(scale[:], ps[:, 0, 0:3], 1.0 / (2 * F * OD), None, ALU.mult).then_inc(total_read, 1)
            dve.wait_ge(total_read, 1)
            nc.vector.tensor_scalar(thr[:], scale[:], 0.5, None, ALU.mult).then_inc(schain, 1)
            nc.vector.tensor_scalar(nthr[:], scale[:], -0.5, None, ALU.mult).then_inc(schain, 1)
            nc.vector.tensor_scalar(gscale[:], scale[:, 0:1], 1.0 / XS, None, ALU.mult).then_inc(schain, 1)
            nc.vector.tensor_scalar(fprod[:], scale[:, 0:1], scale[:, 1:2], 1.0 / HS, ALU.mult, ALU.mult).then_inc(schain, 1)
            dve.wait_ge(schain, 4)
            nc.vector.tensor_scalar(fscale[:], fprod[:], scale[:, 2:3], None, ALU.mult).then_inc(scales_ready, 1)
            normalise(1)
            expand(0, 0, mg)
            for u in range(DC, 2 * DC):
                q_full(u)
            v_full(1)
            x_low(0)
            x_low(1)
            expand(1, 0, mu)
            dve.wait_ge(qr_ready, B * DC)
            dve.wait_ge(q2_ready, B * DC)
            dve.wait_ge(q3_ready, B * DC)

            def hidden(m, b, rows, first=False):
                n = 2 * m + b
                dve.wait_ge(sig_ready, n + 1)
                nc.vector.scalar_tensor_tensor(out=gated[0:rows, b, :], in0=ps[0:rows, 2 * b, :], scalar=HS / (XS * XS),
                                               in1=sig[0:rows, b, :], op0=ALU.mult, op1=ALU.mult).then_inc(gated_ready, 1)
                dve.wait_ge(gated_ready, n + 1)
                dve.wait_ge(up_ready, n + 1)
                if not first:
                    dve.wait_ge(hlo_ready, n - 1)
                nc.vector.tensor_tensor(hid[0:rows, b, :], ps[0:rows, 2 * b + 1, :], gated[0:rows, b, :],
                                        ALU.mult).then_inc(hid_ready, 1)

            for b in range(B):
                hidden(0, b, P, first=True)
            expand(2, 1, md)
            with dve.Fori(1, MF - 1) as m:
                for b in range(B):
                    hidden(m, b, P)
            for b in range(B):
                hidden(MF - 1, b, FL)

            dve.wait_ge(xb_ready, 1)
            with dve.Fori(0, NT // 2) as i:
                for o in range(2):
                    dve.wait_ge(down_ready, 2 * i + o + 1)
                    row = x_sb[:, bass.ds(2 * i + o, 1), :].squeeze(1)
                    nc.vector.scalar_tensor_tensor(out=row, in0=ps[:, 6 + o, :], scalar=fscale[:, 0:1], in1=row,
                                                   op0=ALU.mult, op1=ALU.add).then_inc(down_used, 1)

            def step(i, o, what):
                if "r" in what:
                    g, par = group(i, o + 2), o % 2
                    dve.wait_ge(mt_ready, g + 1)
                    if "s" in what:
                        dve.wait_ge(mrow_st[par], 16 * (i + o // 2 + 1))
                    nc.vector.tensor_copy(mrows[:, par, :], ps[0:2 * GH * TT, 7, 0:P // 2].bitcast(BF16)).then_inc(mt_read, 1)
                if "m" in what:
                    g, par = group(i, o + 3), (o + 3) % 2
                    for n, (t, heads, per) in enumerate(UNITS):
                        keys = (t + 1) * P
                        nb = len(heads) // per
                        dve.wait_ge(rows_ready, NU * g + n + 1)
                        src = ps[:, 2 * (n % 2):2 * (n % 2) + nb, 0:per * keys].rearrange("p b (h k) -> p (b h) k", h=per) \
                            if nb == 1 or per * keys == 512 else ps[:, 2 * (n % 2):2 * (n % 2) + nb, 0:keys]
                        nc.vector.tensor_reduce(negm[:, par, heads[0]:heads[-1] + 1, t], src, axis=AX.X, op=ALU.max,
                                                negate=True).then_inc(rows_used, 1)
                    dve.wait_ge(rows_used, NU * (g + 1))
                    if "e" in what:
                        dve.wait_ge(mt_ready, g - 1)
                    flat = negm[:, par].rearrange("p h t -> p (h t)")
                    nc.vector.tensor_copy(mparts[:, par, 0, :], flat).then_inc(m1_ready, 1)
                    dve.wait_ge(m1_ready, g + 1)
                    nc.vector.tensor_tensor(mparts[:, par, 1, :], flat, mparts[:, par, 0, :],
                                            ALU.subtract).then_inc(mparts_ready, 1)
                if "s" in what:
                    g = group(i, o)
                    dve.wait_ge(sums_ready, g + 1)
                    sums = ps[:, 6, 0:TT * GH * VW].rearrange("p (t h e) -> p t h e", t=TT, h=GH)
                    nc.vector.reciprocal(rden[:], sums[:, :, :, HD]).then_inc(rden_ready, 1)
                    dve.wait_ge(rden_ready, g + 1)
                    dst = attn[:, bass.ds((g // GB) * TT, TT), bass.ds((g % GB) * GH * HD, GH * HD)]
                    nc.vector.tensor_tensor(dst.rearrange("p t (h d) -> p t h d", h=GH), sums[:, :, :, 0:HD],
                                            rden[:].unsqueeze(3).to_broadcast([P, TT, GH, HD]), ALU.mult).then_inc(normed, 1)

            for st in STEPS:
                if st == "loop":
                    with dve.Fori(*LOOPED) as i:
                        for o in range(2):
                            step(i, o, "mresw")
                else:
                    step(*st)

            for t in range(NT):
                dve.wait_ge(o_ready, t + 1)
                nc.vector.tensor_tensor(x_sb[:, t, :], ps[:, 2 + t % 2, :], x_sb[:, t, :], ALU.add).then_inc(y_ready, 1)

        @block.tensor
        def _(pe):
            pe.wait_ge(consts, 4)

            def transposes(n):
                pe.wait_ge(xn_ready, n + 1)
                if n >= 2:
                    pe.wait_ge(xnT_ready, n - 1)
                    pe.wait_ge(xhi_ready, n - 1)
                for c in range(DC):
                    last = nc.tensor.transpose(ps[:, n % 2, c * P:(c + 1) * P], xn[:, n % 2, c * P:(c + 1) * P], identf[:])
                last.then_inc(xt_ready, 1)

            def projections(b):
                t = slice(b * T, (b + 1) * T)
                pe.wait_ge(xnT_ready, (b + 1) * TT)
                pe.wait_ge(wq_ld, 16)
                for m in range(DC):
                    if b:
                        pe.wait_ge(q1_ready, m + 1)
                        pe.wait_ge(qf_ready, m + 1)
                    for c in range(DC):
                        last = nc.tensor.matmul(ps[:, 2 + m, :], wq_sb[:, c, m * P:(m + 1) * P], xnT[:, c, t],
                                                start=c == 0, stop=c == DC - 1)
                    last.then_inc(q_ready, 1)
                pe.wait_ge(wkv_ld, 32)
                if b:
                    pe.wait_ge(kf_ready, b)
                    pe.wait_ge(vsb_ready, b)
                for c in range(DC):
                    last = nc.tensor.matmul(ps[0:BANDS, 6, :], wk_sb[:, c, :], xnT[:, c, t], start=c == 0, stop=c == DC - 1)
                last.then_inc(k_ready, 1)
                for i in range(TT):
                    for c in range(DC):
                        last = nc.tensor.matmul(ps[:, 7, i * HD:(i + 1) * HD], xnT[:, c, b * T + i * P:b * T + (i + 1) * P],
                                                wv_sb[:, c, :], start=c == 0, stop=c == DC - 1)
                last.then_inc(v_ready, 1)

            for n in range(TT):
                transposes(n)
            projections(0)
            pe.wait_ge(wsum_ready, 3)
            nc.tensor.matmul(ps[:, 0, 0:3], ones[:], wsum[:], start=True, stop=True).then_inc(total_ready, 1)
            pe.wait_ge(total_read, 1)
            for n in range(TT, NT):
                transposes(n)
            projections(1)

            pe.wait_ge(xlo_ready, 2)
            pe.wait_ge(built, 2)
            pe.wait_ge(q1_ready, B * DC)
            pe.wait_ge(qf_ready, B * DC)

            def hidden(m, b, rows, first=False):
                n = 2 * m + b
                t = slice(b * T, (b + 1) * T)
                if not first:
                    pe.wait_ge(hid_ready, n - 1)
                for w, bank, ready in ((mg, 2 * b, gate_ready), (mu, 2 * b + 1, up_ready)):
                    for c in range(DC):
                        for h, xh in enumerate((xhi, xlo)):
                            last = nc.tensor.matmul(ps[0:rows, bank, :], w[:, c, bass.ds(m * P, rows)], xh[:, c, t],
                                                    start=c == 0 and h == 0, stop=c == DC - 1 and h == 1)
                    last.then_inc(ready, 1)

            for b in range(B):
                hidden(0, b, P, first=True)
            with pe.Fori(1, MF - 1) as m:
                for b in range(B):
                    hidden(m, b, P)
            for b in range(B):
                hidden(MF - 1, b, FL)

            pe.wait_ge(built, 3)
            for m in range(MF):
                rows = P if m < MF - 1 else FL
                if m >= 2:
                    pe.wait_ge(mdT_ready, m - 1)
                for c in range(DC):
                    last = nc.tensor.transpose(ps[0:rows, 4 + m % 2, c * P // 2:(c + 1) * P // 2].bitcast(FP16),
                                               md[:, c, m * P:m * P + rows], ident16[:])
                last.then_inc(mdt_ready, 1)

            pe.wait_ge(mdT_ready, MF)
            pe.wait_ge(hlo_ready, 2 * MF)
            pe.wait_ge(hhi_ready, 2 * MF)
            pe.wait_ge(kf_ready, B)
            pe.wait_ge(vsb_ready, B)

            def down(i, o, first=False):
                tile = 2 * i + o
                if not first:
                    pe.wait_ge(down_used, tile - 1)
                for m in range(MF):
                    rows = P if m < MF - 1 else FL
                    for h in range(2):
                        last = nc.tensor.matmul(ps[:, 6 + o, :], hbuf[0:rows, h, m, bass.ds(tile * P, P)], mdT[0:rows, m, :],
                                                start=m == 0 and h == 0, stop=m == MF - 1 and h == 1)
                last.then_inc(down_ready, 1)

            down(0, 0, first=True)
            down(0, 1, first=True)
            with pe.Fori(1, NT // 2) as i:
                for o in range(2):
                    down(i, o)
            pe.wait_ge(down_used, NT)
            pe.wait_ge(kchain, 9 * B)

            def step(i, o, what):
                for s, (kc, t) in enumerate(BLOCKS):
                    if "r" in what and s == 1:
                        g, par = group(i, o + 2), o % 2
                        pe.wait_ge(mparts_ready, g + 1)
                        if "e" in what:
                            pe.wait_ge(mt_read, g)
                        nc.tensor.transpose(ps[0:2 * GH * TT, 7, 0:P // 2].bitcast(BF16),
                                            mparts[:, par].rearrange("p a s -> p (a s)"), identb[:]).then_inc(mt_ready, 1)
                    if "m" in what and s in UNIT_AT:
                        g, n = group(i, o + 3), UNIT_AT[s]
                        if s == 0:
                            pe.wait_ge(stack_ld[(o + 3) % 2], 16 * len(PAIRS) * (i + (o + 3) // 2 + 1))
                        if "r" in what or n >= 2:
                            pe.wait_ge(rows_used, NU * g + n - 1)
                        ut, heads, per = UNITS[n]
                        keys = (ut + 1) * P
                        for at in range(len(heads) // per):
                            bank = 2 * (n % 2) + at
                            diag = ps[:, bank, 0:per * keys].rearrange("p (h k) -> p h k", h=per)[:, :, keys - P:keys]
                            nc.tensor.matmul(diag, identb[:], maskq[:].unsqueeze(1).to_broadcast([P, per, P]),
                                             start=True, stop=False, skip_group_check=True)
                            for a in range(per):
                                h = heads[at * per + a]
                                last = nc.tensor.matmul(
                                    ps[:, bank, a * keys:(a + 1) * keys],
                                    qstack[0:BANDS, bass.ds((g % SLOTS) * GW + h * T + ut * P, P)],
                                    kstack[0:BANDS, bass.ds((g // GB) * T, keys)],
                                    start=False, stop=a == per - 1, skip_group_check=True)
                        last.then_inc(rows_ready, 1)
                    if "e" in what:
                        g = group(i, o + 1)
                        if s == 0:
                            pe.wait_ge(mrow_ld[(o + 1) % 2], 16 * (i + (o + 1) // 2 + 1))
                        if "s" in what or s >= 2:
                            pe.wait_ge(exp_ready, NBLK * g + s - 1)
                        qs = qstack[:, bass.ds((g % SLOTS) * GW, GW)].rearrange("r (h q) -> r h q", h=GH)
                        nc.tensor.matmul(ps[:, 4 + s % 2, :].rearrange("p (h q) -> p h q", h=GH),
                                         kstack[:, bass.ds((g // GB) * T + kc * P, P)], qs[:, :, t * P:(t + 1) * P],
                                         start=True, stop=True).then_inc(cols_ready, 1)
                    if "s" in what:
                        g, par = group(i, o), o % 2
                        if s == 0:
                            pe.wait_ge(exp_ready, NBLK * (g + 1))
                            pe.wait_ge(cut_ready, TT * (g + 1))
                            if "w" in what:
                                pe.wait_ge(normed, g)
                        for qt, h in SUMS_AT[s]:
                            at = (qt * GH + h) * VW
                            for kt in range(qt + 1):
                                last = nc.tensor.matmul(ps[:, 6, at:at + VW],
                                                        probs[:, par, BLOCKS.index((kt, qt)), h * P:(h + 1) * P],
                                                        v_sb[:, bass.ds((g // GB) * TT + kt, 1), :].squeeze(1),
                                                        start=kt == 0, stop=kt == qt)
                if "s" in what:
                    last.then_inc(sums_ready, 1)

            for st in STEPS:
                if st == "loop":
                    with pe.Fori(*LOOPED) as i:
                        for o in range(2):
                            step(i, o, "mresw")
                else:
                    step(*st)

            pe.wait_ge(normed, NG)
            pe.wait_ge(rows_used, NU * NG)
            pe.wait_ge(wo_ld, 16)

            def attention_transposes(t):
                if t >= 2:
                    pe.wait_ge(attnT_ready, t - 1)
                for c in range(DC):
                    last = nc.tensor.transpose(ps[:, t % 2, c * P:(c + 1) * P], attn[:, t, c * P:(c + 1) * P], identf[:])
                last.then_inc(at_ready, 1)

            attention_transposes(0)
            for t in range(NT):
                if t + 1 < NT:
                    attention_transposes(t + 1)
                pe.wait_ge(attnT_ready, t + 1)
                if t >= 2:
                    pe.wait_ge(y_ready, t - 1)
                for c in range(DC):
                    last = nc.tensor.matmul(ps[:, 2 + t % 2, :], attnT[:, t % 2, c, :], wo_sb[:, c, :],
                                            start=c == 0, stop=c == DC - 1)
                last.then_inc(o_ready, 1)


def octonion_signs():
    s = np.zeros((J, J, J), np.float32)
    s[0, 0, 0] = 1.0
    for i in range(1, J):
        s[0, i, i] = s[i, 0, i] = 1.0
        s[i, i, 0] = -1.0
    for a, b, c in [(1, 2, 3), (1, 4, 5), (1, 7, 6), (2, 4, 6), (2, 5, 7), (3, 4, 7), (3, 6, 5)]:
        for p, q, r in ((a, b, c), (b, c, a), (c, a, b)):
            s[p, q, r], s[q, p, r] = 1.0, -1.0
    return s


def slots(w, component_last):
    w = w.transpose(0, 2, 1) if component_last else w
    halves = [w[[j ^ h for j in range(J)]].transpose(1, 0, 2).reshape(OD, F) for h in range(2)]
    return np.ascontiguousarray(np.concatenate(halves, 0))


def kernel(**inputs):
    import concourse.bacc as bacc
    from concourse.bass_utils import run_bass_kernel_spmd

    a = {k.replace("L0_", ""): np.asarray(v) for k, v in inputs.items()}
    s = octonion_signs()
    signs = np.zeros((P, 2, DC, J), np.float32)
    for c in range(DC):
        for h in range(2):
            for k in range(J):
                rows = slice(h * OD, (h + 1) * OD)
                i = 2 * c + h
                signs[rows, 0, c, k] = s[i ^ k, i, k]
                signs[rows, 1, c, k] = s[i ^ k, k, i]
    bands = np.zeros((BANDS, 3), np.float32)
    for r, (_, part) in enumerate(PAIRS):
        bands[r * HD:(r + 1) * HD, part] = 1.0
    arrays = {
        "x": a["attn_x"].reshape(TOK, D),
        "wqT": a["attn_wq_w"].T,
        "wkT": np.tile(a["attn_wk_w"].T, (1, len(PAIRS))),
        "wvT": a["attn_wv_w"].T,
        "woT": a["attn_wo_w"].T,
        "bq": a["attn_wq_b"].reshape(DC, P).T,
        "bk": np.tile(a["attn_wk_b"], len(PAIRS)).reshape(BANDS, 1),
        "bv": a["attn_wv_b"],
        "bo": a["attn_wo_b"],
        "wg": slots(a["ffn_w_gate"], True),
        "wu": slots(a["ffn_w_up"], True),
        "wd": slots(a["ffn_w_down"], False),
        "signs": signs.reshape(P, 2 * DC * J),
        "bands": bands,
    }
    arrays = {k: np.ascontiguousarray(v) for k, v in arrays.items()}
    nc = bacc.Bacc("TRN2", target_bir_lowering=False, num_devices=1)
    args = [nc.dram_tensor(k, v.shape, mybir.dt.from_np(v.dtype), kind="ExternalInput").ap() for k, v in arrays.items()]
    out = nc.dram_tensor("out", (TOK, D), FP32, kind="ExternalOutput").ap()
    build(nc, *args, out)
    r = run_bass_kernel_spmd(nc, [arrays], core_ids=[0])
    return r.results[0]["out"].reshape(a["attn_x"].shape)
```

```python
import numpy as np
import concourse.bass as bass
from concourse import mybir
from contextlib import ExitStack

FP32 = mybir.dt.float32
BF16 = mybir.dt.bfloat16
FP16 = mybir.dt.float16
ALU = mybir.AluOpType
ACT = mybir.ActivationFunctionType
AX = mybir.AxisListType

P = 128
B, T, D = 2, 512, 512
TOK = B * T
NT = TOK // P
TT = T // P
DC = D // P
H, HD = 32, 16
VW = 3 * HD + 1
SW = 64
J, OD, HID = 8, D // 8, 170
F = J * HID
MF = -(-F // P)
FL = F - (MF - 1) * P
GH = 4
NG = B * H // GH
GB = NG // B
GW = GH * T
PAIRS = [(0, 0), (0, 1), (0, 2), (1, 0), (1, 1), (2, 0)]
BANDS = len(PAIRS) * HD
ROWS = BANDS + 2
KV = BANDS + HD
QSLOTS = 4
SLOTS = 4
BLOCKS = [(kc, t) for t in range(TT) for kc in range(t + 1)]
NBLK = len(BLOCKS)
UNITS = [(1, (0, 1, 2, 3), 2), (0, (0, 1, 2, 3), 4), (2, (0, 1), 1), (2, (2, 3), 1), (3, (0, 1), 1), (3, (2, 3), 1)]
NU = len(UNITS)
UNIT_AT = {0: 0, 2: 1, 3: 2, 5: 3, 7: 4, 9: 5}
UNIT_BLOCKS = list(UNIT_AT)
DOWN_AT = (0, 2, 5, 7)
DOWN_TILES = len(DOWN_AT)
OUT_TILES = 2
OUT_AT = {3: [(0, 0)], 4: [(0, 1)], 5: [(0, 2)], 6: [(0, 3)], 7: [(1, 0)], 8: [(1, 1)], 9: [(1, 2), (1, 3)]}
TRANSPOSED_AT, COPIED_AT = (1, 5), (3, 7)
SUMS_AT = [[], [], [(2, 0), (2, 1)], [(2, 2), (2, 3)], [(3, 0)], [(3, 1)], [(3, 2)], [(3, 3), (1, 0)],
           [(1, 1), (1, 2)], [(1, 3), (0, 0), (0, 1), (0, 2), (0, 3)]]
FIRST_SUMS, FIRST_TILE_3, FIRST_LOW_TILES = (min(s for s, sums in enumerate(SUMS_AT) if any(t in tiles for t, _ in sums))
                                             for tiles in ((0, 1, 2, 3), (3,), (0, 1)))
LAST_SUMS = [[(t, h) for sums in SUMS_AT for t, h in sums if t // 2 == u][-1] for u in range(2)]
LAST_BLOCK = [max(s for s, (_, u) in enumerate(BLOCKS) if u == t) for t in range(TT)]
MAXIMA_AT = 2
MAXIMA_BANK = 3
COPIED_AFTER = 1
LOW_DVE = (3, 6)
LOW_AFTER = (2, 4)
LOW_POOL = [s for s in range(NBLK) if s not in LOW_DVE]
EPS = 1e-5
XS = 1024.0
HS = 0.125
PS = 1024.0
MASKED = -1e30


def build(nc, x, wqT, wkvT, woT, bq, bkv, bo, wg, wu, wd, signs, bands, out):
    ctx = ExitStack()
    with ctx:
        def sb(name, shape, dt=FP32):
            return ctx.enter_context(nc.sbuf_tensor(name, shape, dt))

        def sem(name):
            return ctx.enter_context(nc.semaphore(name))

        x_sb = sb("x_sb", [P, NT, D])
        xn = sb("xn", [P, TT, D])
        attnT = xn[:, 0:2, :].rearrange("p s (c q) -> p s c q", c=DC)
        xnT = sb("xnT", [P, DC, TOK])
        mdT = xnT[:].rearrange("p c t -> p (c t)").bitcast(FP16)[:, 0:MF * D].rearrange("p (m n) -> p m n", m=MF)
        attn = xnT[:].rearrange("p c t -> p (c t)").rearrange("p (t n) -> p t n", t=NT)
        xhi = sb("xhi", [P, DC, TOK], FP16)
        xlo = sb("xlo", [P, DC, TOK], FP16)
        wq_sb = sb("wq_sb", [P, DC, D])
        wkv_sb = sb("wkv_sb", [P, DC, KV])
        wo_sb = sb("wo_sb", [P, DC, D])
        bq_sb = sb("bq_sb", [P, DC])
        bkv_sb = sb("bkv_sb", [KV, 1])
        bo_sb = sb("bo_sb", [P, D])
        signs_sb = sb("signs_sb", [P, 2, DC, J])
        bands_sb = sb("bands_sb", [BANDS, 3])
        raw = sb("raw", [P, max(3 * F, SLOTS * GW // 2)])
        qstack = raw[0:ROWS, 0:SLOTS * GW // 2].bitcast(BF16)
        neg = sb("neg", [P, F], FP16)
        tern = sb("tern", [P, F], FP16)
        mgu = sb("mgu", [P, 2, DC, F], FP16)
        mg, mu = mgu[:, 0], mgu[:, 1]
        full = mgu[:].rearrange("p w c f -> p (w c f)").bitcast(FP32)[:, 0:NBLK * GH * P].rearrange("p (s n) -> p s n", s=NBLK)
        md = sb("md", [P, DC, F], FP16)
        hbuf = sb("hbuf", [P, 2, MF, TOK], FP16)
        probs = hbuf[:, :, 0:NBLK, :].rearrange("p g n (a c) -> p g n a c", a=2)
        under = hbuf[:, 1].rearrange("p m t -> p (m t)").bitcast(BF16)
        qpart = under[:, 0:12 * T].rearrange("p (r s t) -> p r s t", r=3, s=QSLOTS)
        kpart = under[0:BANDS, 12 * T:15 * T].rearrange("p (r t) -> p r t", r=3)
        kband = under[0:BANDS, 15 * T:18 * T].rearrange("p (r t) -> p r t", r=3)
        kstack = sb("kstack", [ROWS, TOK], BF16)
        v_sb = sb("v_sb", [P, NT, VW], BF16)
        vf = sb("vf", [P, TT, HD])
        vr = sb("vr", [P, TT, HD])
        osum = sb("osum", [P, TT, GH, HD])
        sig = sb("sig", [P, 2, T])
        gated = sb("gated", [P, 2, T])
        hid = sb("hid", [P, 2, T])
        kvf = sig[0:KV, 0, :]
        kf, kr = sig[0:BANDS, 0, :], sig[0:BANDS, 1, :]
        qf, qr = gated, hid
        stats = sb("stats", [P, NT, 6])
        mv = sb("mv", [P, NT, 2])
        vare = sb("vare", [P, NT])
        half = sb("half", [P, NT])
        rstd = sb("rstd", [P, NT])
        wsum = sb("wsum", [P, 3])
        scale = sb("scale", [P, 3])
        thr = sb("thr", [P, 3])
        nthr = sb("nthr", [P, 3])
        gscale = sb("gscale", [P, 1])
        fprod = sb("fprod", [P, 1])
        fscale = sb("fscale", [P, 1])
        ones = sb("ones", [P, P])
        identf = sb("identf", [P, P])
        ident16 = sb("ident16", [P, P], FP16)
        identb = sb("identb", [P, P], BF16)
        maskq = sb("maskq", [P, P], BF16)
        maskk = sb("maskk", [P, P], BF16)
        negm = sb("negm", [P, 2, GH, TT])
        mparts = sb("mparts", [P, 2, 2, GH * TT], BF16)
        mrows = sb("mrows", [2 * GH * TT, 2, P], BF16)
        rden = sb("rden", [P, TT, GH])
        ps = ctx.enter_context(nc.psum_tensor("ps", [P, 8, 512], FP32))
        q_dram = nc.dram_tensor("q_parts", [3, D, TOK], BF16, kind="Internal").ap()

        m_dram = nc.dram_tensor("minus_maxima", [NG, 2 * GH * TT, P], BF16, kind="Internal").ap()

        x_ld = [sem(f"x_ld{i}") for i in range(NT // 2)]
        wq_ld, wkv_ld, wo_ld, small_ld = sem("wq_ld"), sem("wkv_ld"), sem("wo_ld"), sem("small_ld")
        raw_ld = [sem(f"raw_ld{i}") for i in range(3)]
        filled, consts = sem("filled"), sem("consts")
        stats_done, mv_done, vare_ready, rstd_ready = sem("stats_done"), sem("mv_done"), sem("vare_ready"), sem("rstd_ready")
        xn_ready, xt_ready, xnT_ready, xhi_ready, xlo_ready = (sem("xn_ready"), sem("xt_ready"), sem("xnT_ready"),
                                                               sem("xhi_ready"), sem("xlo_ready"))
        xb_ready = sem("xb_ready")
        q_ready, q1_ready, qf_ready, qr_ready, q2_ready, q3_ready = (sem("q_ready"), sem("q1_ready"), sem("qf_ready"),
                                                                     sem("qr_ready"), sem("q2_ready"), sem("q3_ready"))
        q_out = [sem(f"q_out{i}") for i in range(QSLOTS)]
        k_ready, kf_ready, k1_ready, kr_ready, k2_ready, k3_ready = (sem("k_ready"), sem("kf_ready"), sem("k1_ready"),
                                                                     sem("kr_ready"), sem("k2_ready"), sem("k3_ready"))
        kband_ready, ksum_ready, kstack_ready = sem("kband_ready"), sem("ksum_ready"), sem("kstack_ready")
        v_ready, vsb_ready = sem("v_ready"), sem("vsb_ready")
        wsum_ready, total_ready, total_read, schain, scales_ready = (sem("wsum_ready"), sem("total_ready"), sem("total_read"),
                                                                     sem("schain"), sem("scales_ready"))
        neg_done, tern_done, built = sem("neg_done"), sem("tern_done"), sem("built")
        gate_ready, up_ready, sig_ready, gated_ready = sem("gate_ready"), sem("up_ready"), sem("sig_ready"), sem("gated_ready")
        hid_ready, hhi_ready, hlo_ready = sem("hid_ready"), sem("hhi_ready"), sem("hlo_ready")
        mdt_ready, down_ready, down_used = sem("mdt_ready"), sem("down_ready"), sem("down_used")
        mdT_ready = [sem("mdT_ready_act"), sem("mdT_ready_dve")]
        stack_ld = [sem("stack_ld0"), sem("stack_ld1")]
        mrow_st = [sem("mrow_st0"), sem("mrow_st1")]
        mrow_ld = [sem("mrow_ld0"), sem("mrow_ld1")]
        rows_ready, rows_used, m1_ready, mparts_ready = sem("rows_ready"), sem("rows_used"), sem("m1_ready"), sem("mparts_ready")
        mt_ready, mt_read, cols_ready, exp_ready = sem("mt_ready"), sem("mt_read"), sem("cols_ready"), sem("exp_ready")
        high_ready, low_ready, plow_ready = sem("high_ready"), sem("low_ready"), sem("plow_ready")
        vchain = sem("vchain")
        rden_ready = sem("rden_ready")
        sums_ready, osum_ready, normed = ([sem(f"{name}{u}") for u in range(2)] for name in ("sums_ready", "osum_ready", "normed"))
        at_ready, attnT_ready, o_ready, y_ready, y_out = (sem("at_ready"), sem("attnT_ready"), sem("o_ready"), sem("y_ready"),
                                                          sem("y_out"))

        block = ctx.enter_context(nc.Block())

        STEPS = [(-1, -1, "md"), (-1, 0, "mrd"), (-1, 1, "mre"), (0, 0, "mres"), (0, 1, "mreswp"), "loop",
                 (6, 0, "mreswp"), (6, 1, "reswpo"), (6, 2, "eswpo"), (6, 3, "swp")]
        LOOPED = (1, 6)

        def group(i, o):
            return 2 * i + o

        @block.sync
        def _(sp):
            x_t = x.rearrange("(n p) d -> p n d", p=P)
            for i in range(2):
                sp.dma_start(x_sb[:, 2 * i:2 * i + 2, :], x_t[:, 2 * i:2 * i + 2, :]).then_inc(x_ld[i], 16)
            sp.dma_start(wq_sb[:], wqT.rearrange("(c p) n -> p c n", p=P)).then_inc(wq_ld, 16)
            for i in range(2, 4):
                sp.dma_start(x_sb[:, 2 * i:2 * i + 2, :], x_t[:, 2 * i:2 * i + 2, :]).then_inc(x_ld[i], 16)
            for i, w in enumerate((wg, wu, wd)):
                sp.dma_start(raw[:, i * F:(i + 1) * F], w).then_inc(raw_ld[i], 16)
            sp.dma_start(wo_sb[:], woT.rearrange("(c p) n -> p c n", p=P)).then_inc(wo_ld, 16)
            for u in range(B * DC):
                b, m, s = u // DC, u % DC, u % QSLOTS
                sp.wait_ge(q1_ready, u + 1)
                sp.wait_ge(q2_ready, u + 1)
                sp.wait_ge(q3_ready, u + 1)
                sp.dma_start(q_dram[:, m * P:(m + 1) * P, b * T:(b + 1) * T].rearrange("r p t -> p r t"),
                             qpart[:, :, s, :]).then_inc(q_out[s], 16)

            def load_stack(i, o):
                g = group(i, o)
                for r, (part, _) in enumerate(PAIRS):
                    sp.dma_start(
                        qstack[r * HD:(r + 1) * HD, bass.ds((g % SLOTS) * GW, GW)].rearrange("d (h t) -> d h t", h=GH),
                        q_dram[part, bass.ds((g % GB) * GH * HD, GH * HD), bass.ds((g // GB) * T, T)]
                        .rearrange("(h d) t -> d h t", d=HD)).then_inc(stack_ld[o % 2], 16)

            def load_maxima(i, o):
                g = group(i, o)
                sp.wait_ge(mt_read, g + 1)
                sp.dma_start(m_dram[bass.ds(g, 1)].squeeze(0), mrows[:, o % 2, :]).then_inc(mrow_st[o % 2], 16)
                sp.wait_ge(mrow_st[o % 2], 16 * (i + o // 2 + 1))
                sp.dma_start(qstack[BANDS:ROWS, bass.ds((g % SLOTS) * GW, GW)],
                             m_dram[bass.ds(g, 1)].squeeze(0).rearrange("(r s) q -> r (s q)", r=2)).then_inc(mrow_ld[o % 2], 16)

            for s in range(QSLOTS):
                sp.wait_ge(q_out[s], 16 * B * DC // QSLOTS)
            sp.wait_ge(tern_done, 3)
            load_stack(0, 0)
            load_stack(0, 1)
            sp.wait_ge(stack_ld[0], 16 * len(PAIRS))
            load_stack(0, 2)
            sp.wait_ge(stack_ld[1], 16 * len(PAIRS))
            load_stack(0, 3)

            def step(i, o, what, stack):
                if stack:
                    sp.wait_ge(cols_ready, NBLK * (group(i, o) + 1))
                    load_stack(i, o + 4)
                if "r" in what:
                    load_maxima(i, o + 2)

            for st in STEPS:
                if st == "loop":
                    with sp.Fori(*LOOPED) as i:
                        for o in range(2):
                            step(i, o, "mreswp", True)
                else:
                    step(*st, st[0] == 0)

            out_t = out.rearrange("(n p) d -> p n d", p=P)
            for t in range(NT):
                sp.wait_ge(y_ready, t + 1)
                sp.dma_start(out_t[:, t, :], x_sb[:, t, :]).then_inc(y_out, 16)
            sp.wait_ge(y_out, 16 * NT)

        @block.gpsimd
        def _(pool):
            for m in (identf, ident16, identb, maskq, maskk):
                nc.gpsimd.memset(m[:], 0.0).then_inc(filled, 1)
            nc.gpsimd.memset(ones[:], 1.0).then_inc(filled, 1)
            nc.gpsimd.memset(half[:], -0.5).then_inc(filled, 1)
            nc.gpsimd.memset(v_sb[:, :, VW - 1:VW], 1.0).then_inc(filled, 1)
            pool.wait_ge(filled, 8)
            nc.gpsimd.memset(kstack[BANDS:ROWS, :], 1.0).then_inc(filled, 1)
            pool.wait_ge(filled, 9)
            for m in (identf, ident16, identb):
                nc.gpsimd.affine_select(out=m[:], in_=m[:], compare_op=ALU.not_equal, fill=1.0, base=0,
                                        pattern=[[-1, P]], channel_multiplier=1).then_inc(consts, 1)
            nc.gpsimd.affine_select(out=maskq[:], in_=maskq[:], compare_op=ALU.is_ge, fill=MASKED, base=0,
                                    pattern=[[-1, P]], channel_multiplier=1).then_inc(consts, 1)
            nc.gpsimd.affine_select(out=maskk[:], in_=maskk[:], compare_op=ALU.is_ge, fill=MASKED, base=0,
                                    pattern=[[1, P]], channel_multiplier=-1).then_inc(consts, 1)

            def rsqrt(b):
                pool.wait_ge(vare_ready, b + 1)
                t = slice(b * TT, (b + 1) * TT)
                nc.gpsimd.tensor_tensor(rstd[:, t], vare[:, t], half[:, t], ALU.pow).then_inc(rstd_ready, 1)

            def q_rest(u):
                s = u % 2
                pool.wait_ge(qf_ready, u + 1)
                pool.wait_ge(q1_ready, u + 1)
                if u >= 2:
                    pool.wait_ge(q2_ready, u - 1)
                    pool.wait_ge(q3_ready, u - 1)
                nc.gpsimd.tensor_tensor(qr[:, s, :], qf[:, s, :], qpart[:, 0, u % QSLOTS, :], ALU.subtract).then_inc(qr_ready, 1)

            def q_third(u):
                pool.wait_ge(qr_ready, u + 1)
                pool.wait_ge(q2_ready, u + 1)
                nc.gpsimd.tensor_tensor(qpart[:, 2, u % QSLOTS, :], qr[:, u % 2, :], qpart[:, 1, u % QSLOTS, :],
                                        ALU.subtract).then_inc(q3_ready, 1)

            def k_rest(b):
                pool.wait_ge(k1_ready, b + 1)
                nc.gpsimd.tensor_tensor(kr, kf, kpart[:, 0, :], ALU.subtract).then_inc(kr_ready, 1)

            def k_third(b):
                pool.wait_ge(kr_ready, b + 1)
                pool.wait_ge(k2_ready, b + 1)
                nc.gpsimd.tensor_tensor(kpart[:, 2, :], kr, kpart[:, 1, :], ALU.subtract).then_inc(k3_ready, 1)

            def k_bands(b):
                pool.wait_ge(kband_ready, 3 * (b + 1))
                nc.gpsimd.tensor_tensor(kband[:, 0, :], kband[:, 0, :], kband[:, 1, :], ALU.add).then_inc(ksum_ready, 1)
                pool.wait_ge(ksum_ready, b + 1)
                nc.gpsimd.tensor_tensor(kstack[0:BANDS, b * T:(b + 1) * T], kband[:, 0, :], kband[:, 2, :],
                                        ALU.add).then_inc(kstack_ready, 1)

            rsqrt(0)
            rsqrt(1)
            q_rest(0)
            q_rest(1)
            q_third(0)
            k_rest(0)
            q_third(1)
            q_rest(2)
            k_third(0)
            q_rest(3)
            q_third(2)
            k_bands(0)
            k_rest(1)
            q_third(3)
            q_rest(4)
            k_third(1)
            q_rest(5)
            q_third(4)
            k_bands(1)
            for u in range(6, B * DC):
                q_rest(u)
                q_third(u - 1)
            q_third(B * DC - 1)
            pool.wait_ge(small_ld, 16 * 5)
            pool.wait_ge(xn_ready, NT)
            nc.gpsimd.tensor_tensor(x_sb[:], x_sb[:], bo_sb[:].unsqueeze(1).to_broadcast([P, NT, D]),
                                    ALU.add).then_inc(xb_ready, 1)

            def hidden_low(m, b, rows):
                n = 2 * m + b
                pool.wait_ge(hid_ready, n + 1)
                pool.wait_ge(hhi_ready, n + 1)
                cols = slice(b * T, (b + 1) * T)
                nc.gpsimd.tensor_tensor(hbuf[0:rows, 1, bass.ds(m, 1), cols].squeeze(1), hid[0:rows, b, :],
                                        hbuf[0:rows, 0, bass.ds(m, 1), cols].squeeze(1), ALU.subtract).then_inc(hlo_ready, 1)

            for s in range(QSLOTS):
                pool.wait_ge(q_out[s], 16 * B * DC // QSLOTS)
            with pool.Fori(0, MF - 1) as m:
                for b in range(B):
                    hidden_low(m, b, P)
            for b in range(B):
                hidden_low(MF - 1, b, FL)

            def step(i, o, what):
                if "e" not in what:
                    return
                e, par = group(i, o + 1), (o + 1) % 2
                for s in LOW_POOL:
                    pool.wait_ge(high_ready, NBLK * e + s + 1)
                    nc.gpsimd.tensor_tensor(probs[:, par, s, 1, :], full[:, s, :], probs[:, par, s, 0, :],
                                            ALU.subtract).then_inc(plow_ready, 1)

            for st in STEPS:
                if st == "loop":
                    with pool.Fori(*LOOPED) as i:
                        for o in range(2):
                            step(i, o, "mreswp")
                else:
                    step(*st)

        @block.scalar
        def _(act):
            act.dma_start(wkv_sb[:], wkvT.rearrange("(c p) n -> p c n", p=P)).then_inc(wkv_ld, 16)
            act.dma_start(bq_sb[:], bq).then_inc(small_ld, 16)
            act.dma_start(bkv_sb[:], bkv).then_inc(small_ld, 16)
            act.dma_start(bo_sb[:], bo.rearrange("(a n) -> a n", a=1).to_broadcast([P, D])).then_inc(small_ld, 16)
            act.dma_start(signs_sb[:].rearrange("p a c k -> p (a c k)"), signs).then_inc(small_ld, 16)
            act.dma_start(bands_sb[:], bands).then_inc(small_ld, 16)

            def q_first(u):
                s = u % QSLOTS
                act.wait_ge(q_ready, u + 1)
                if u >= QSLOTS:
                    act.wait_ge(q_out[s], 16 * (u // QSLOTS))
                nc.scalar.activation(qpart[:, 0, s, :], ps[:, 2 + u % DC, :], ACT.Identity,
                                     bias=bq_sb[:, u % DC:u % DC + 1]).then_inc(q1_ready, 1)

            def q_second(u):
                act.wait_ge(qr_ready, u + 1)
                nc.scalar.activation(qpart[:, 1, u % QSLOTS, :], qr[:, u % 2, :], ACT.Copy).then_inc(q2_ready, 1)

            def k_first(b):
                act.wait_ge(k_ready, b + 1)
                if b:
                    act.wait_ge(kstack_ready, b)
                    act.wait_ge(v_ready, b)
                nc.scalar.activation(kvf, ps[0:KV, 6, :], ACT.Identity, bias=bkv_sb[:, 0:1]).then_inc(kf_ready, 1)
                act.wait_ge(kf_ready, b + 1)
                nc.scalar.activation(kpart[:, 0, :], kf, ACT.Copy).then_inc(k1_ready, 1)

            def k_second(b):
                act.wait_ge(kr_ready, b + 1)
                nc.scalar.activation(kpart[:, 1, :], kr, ACT.Copy).then_inc(k2_ready, 1)

            def k_masked(b):
                act.wait_ge(k2_ready, b + 1)
                act.wait_ge(k3_ready, b + 1)
                for r in range(3):
                    nc.scalar.activation(kband[:, r, :], kpart[:, r, :], ACT.Copy,
                                         scale=bands_sb[:, r:r + 1]).then_inc(kband_ready, 1)

            for n in range(NT):
                act.wait_ge(xt_ready, n + 1)
                src = ps[:, n % 2, :].rearrange("p (c q) -> p c q", c=DC)
                nc.scalar.activation(xnT[:, :, n * P:(n + 1) * P], src, ACT.Copy).then_inc(xnT_ready, 1)
                nc.scalar.activation(xhi[:, :, n * P:(n + 1) * P], src, ACT.Copy, scale=XS).then_inc(xhi_ready, 1)
            act.wait_ge(small_ld, 16 * 5)
            q_first(0)
            q_first(1)
            q_second(0)
            k_first(0)
            q_second(1)
            q_first(2)
            k_second(0)
            q_first(3)
            q_second(2)
            k_masked(0)
            k_first(1)
            q_second(3)
            q_first(4)
            k_second(1)
            q_first(5)
            q_second(4)
            k_masked(1)
            for u in range(6, B * DC):
                q_first(u)
                q_second(u - 1)
            q_second(B * DC - 1)
            act.wait_ge(kstack_ready, B)
            act.wait_ge(v_ready, B)
            act.wait_ge(scales_ready, 1)

            def hidden(m, b, rows):
                n = 2 * m + b
                cols = slice(b * T, (b + 1) * T)
                act.wait_ge(gate_ready, n + 1)
                nc.scalar.activation(sig[0:rows, b, :], ps[0:rows, 2 * b, :], ACT.Sigmoid,
                                     scale=gscale[0:rows, 0:1]).then_inc(sig_ready, 1)
                act.wait_ge(hid_ready, n + 1)
                nc.scalar.activation(hbuf[0:rows, 0, bass.ds(m, 1), cols].squeeze(1), hid[0:rows, b, :],
                                     ACT.Copy).then_inc(hhi_ready, 1)

            with act.Fori(0, MF - 1) as m:
                for b in range(B):
                    hidden(m, b, P)
            for b in range(B):
                hidden(MF - 1, b, FL)
            for m in range(0, MF, 2):
                rows = P if m < MF - 1 else FL
                act.wait_ge(mdt_ready, m + 1)
                nc.scalar.activation(mdT[0:rows, m, :], ps[0:rows, 4 + m % 4, 0:D // 2].bitcast(FP16),
                                     ACT.Copy).then_inc(mdT_ready[0], 1)

            def copy_transposed(t):
                act.wait_ge(at_ready, t + 1)
                if t >= 2:
                    act.wait_ge(o_ready, t - 1)
                nc.scalar.activation(attnT[:, t % 2], ps[:, t % 2, :].rearrange("p (c q) -> p c q", c=DC),
                                     ACT.Copy).then_inc(attnT_ready, 1)

            def step(i, o, what):
                if "e" not in what:
                    return
                e, par = group(i, o + 1), (o + 1) % 2
                for s in range(NBLK + 1):
                    if "o" in what and s in COPIED_AT:
                        copy_transposed(OUT_TILES * (o - 1) + COPIED_AT.index(s))
                    if s < NBLK:
                        act.wait_ge(cols_ready, NBLK * e + s + 1)
                        if s == 0 and "w" in what:
                            act.wait_ge(sums_ready[0], e - 1)
                        if "s" in what:
                            if s in LOW_DVE:
                                act.wait_ge(low_ready, len(LOW_DVE) * (e - 1) + LOW_DVE.index(s) + 1)
                            else:
                                act.wait_ge(plow_ready, len(LOW_POOL) * (e - 1) + LOW_POOL.index(s) + 1)
                        nc.scalar.activation(full[:, s, :], ps[:, 4 + s % 2, :], ACT.Exp,
                                             scale=float(HD) ** -0.5).then_inc(exp_ready, 1)
                    if s:
                        h = s - 1
                        act.wait_ge(exp_ready, NBLK * e + h + 1)
                        nc.scalar.activation(probs[:, par, h, 0, :], full[:, h, :], ACT.Copy).then_inc(high_ready, 1)

            for st in STEPS:
                if st == "loop":
                    with act.Fori(*LOOPED) as i:
                        for o in range(2):
                            step(i, o, "mreswp")
                else:
                    step(*st)

            for t in range(OUT_TILES * 2, NT):
                copy_transposed(t)

        @block.vector
        def _(dve):
            def statistics(b):
                for n in range(b * TT, (b + 1) * TT):
                    dve.wait_ge(x_ld[n // 2], 16)
                    nc.vector.bn_stats(stats[:, n, :], x_sb[:, n, :]).then_inc(stats_done, 1)
                for n in range(b * TT, (b + 1) * TT):
                    dve.wait_ge(stats_done, n + 1)
                    nc.vector.bn_aggr(mv[:, n, :], stats[:, n, :]).then_inc(mv_done, 1)
                dve.wait_ge(mv_done, (b + 1) * TT)
                t = slice(b * TT, (b + 1) * TT)
                nc.vector.tensor_scalar(vare[:, t], mv[:, t, 1], EPS, None, ALU.add).then_inc(vare_ready, 1)

            def normalise(b):
                dve.wait_ge(rstd_ready, b + 1)
                for n in range(b * TT, (b + 1) * TT):
                    if b:
                        dve.wait_ge(xt_ready, n - TT + 1)
                    nc.vector.tensor_scalar(xn[:, n % TT, :], x_sb[:, n, :], mv[:, n, 0:1], rstd[:, n:n + 1],
                                            ALU.subtract, ALU.mult).then_inc(xn_ready, 1)

            def x_low(b):
                dve.wait_ge(xnT_ready, (b + 1) * TT)
                dve.wait_ge(xhi_ready, (b + 1) * TT)
                t = slice(b * T, (b + 1) * T)
                for c in range(DC):
                    last = nc.vector.scalar_tensor_tensor(out=xlo[:, c, t], in0=xnT[:, c, t], scalar=XS,
                                                          in1=xhi[:, c, t], op0=ALU.mult, op1=ALU.subtract)
                last.then_inc(xlo_ready, 1)

            def q_full(u):
                s = u % 2
                dve.wait_ge(q1_ready, u + 1)
                if u >= 2:
                    dve.wait_ge(qr_ready, u - 1)
                nc.vector.tensor_scalar(qf[:, s, :], ps[:, 2 + u % DC, :], bq_sb[:, u % DC:u % DC + 1], None,
                                        ALU.add).then_inc(qf_ready, 1)

            vlinks = [0]

            def vlink(ins):
                vlinks[0] += 1
                ins.then_inc(vchain, 1)
                dve.wait_ge(vchain, vlinks[0])

            def v_parts(b):
                dve.wait_ge(v_ready, b + 1)
                vp = v_sb[:, b * TT:(b + 1) * TT, 0:3 * HD].rearrange("p t (r d) -> p r t d", r=3)
                vlink(nc.vector.tensor_copy(vf[:].rearrange("p t d -> p (t d)"), ps[:, 7, 0:TT * HD]))
                vlink(nc.vector.tensor_copy(vp[:, 0], vf[:]))
                vlink(nc.vector.tensor_tensor(vr[:], vf[:], vp[:, 0], ALU.subtract))
                vlink(nc.vector.tensor_copy(vp[:, 1], vr[:]))
                nc.vector.tensor_tensor(vp[:, 2], vr[:], vp[:, 1], ALU.subtract).then_inc(vsb_ready, 1)

            def ternary(w):
                cols = slice(w * F, (w + 1) * F)
                if w:
                    dve.wait_ge(built, DC * w)
                nc.vector.tensor_scalar(neg[:], raw[:, cols], nthr[:, w:w + 1], None, ALU.is_lt).then_inc(neg_done, 1)
                dve.wait_ge(neg_done, w + 1)
                nc.vector.scalar_tensor_tensor(out=tern[:], in0=raw[:, cols], scalar=thr[:, w:w + 1], in1=neg[:],
                                               op0=ALU.is_gt, op1=ALU.subtract).then_inc(tern_done, 1)
                dve.wait_ge(tern_done, w + 1)

            def expand(c, kind, dst):
                for k in range(J):
                    j = (2 * c) ^ k
                    last = nc.vector.tensor_scalar(dst[:, c, k * HID:(k + 1) * HID], tern[:, j * HID:(j + 1) * HID],
                                                   signs_sb[:, kind, c, k:k + 1], None, ALU.mult)
                last.then_inc(built, 1)

            statistics(0)
            normalise(0)
            statistics(1)
            normalise(1)
            for w in range(3):
                dve.wait_ge(raw_ld[w], 16)
                nc.vector.tensor_reduce(wsum[:, w:w + 1], raw[:, w * F:(w + 1) * F], axis=AX.X, op=ALU.add,
                                        apply_absolute_value=True).then_inc(wsum_ready, 1)
            dve.wait_ge(small_ld, 16 * 5)
            dve.wait_ge(total_ready, 1)
            nc.vector.tensor_scalar(scale[:], ps[:, 7, 0:3], 1.0 / (2 * F * OD), None, ALU.mult).then_inc(total_read, 1)
            dve.wait_ge(total_read, 1)
            nc.vector.tensor_scalar(thr[:], scale[:], 0.5, None, ALU.mult).then_inc(schain, 1)
            nc.vector.tensor_scalar(nthr[:], scale[:], -0.5, None, ALU.mult).then_inc(schain, 1)
            nc.vector.tensor_scalar(gscale[:], scale[:, 0:1], 1.0 / XS, None, ALU.mult).then_inc(schain, 1)
            nc.vector.tensor_scalar(fprod[:], scale[:, 0:1], scale[:, 1:2], 1.0 / HS, ALU.mult, ALU.mult).then_inc(schain, 1)
            dve.wait_ge(schain, 4)
            nc.vector.tensor_scalar(fscale[:], fprod[:], scale[:, 2:3], None, ALU.mult).then_inc(scales_ready, 1)
            q_full(0)
            ternary(0)
            q_full(1)
            expand(0, 0, mg)
            q_full(2)
            expand(1, 0, mg)
            expand(2, 0, mg)
            q_full(3)
            expand(3, 0, mg)
            v_parts(0)
            x_low(0)
            q_full(4)
            ternary(1)
            expand(0, 0, mu)
            q_full(5)
            expand(1, 0, mu)
            v_parts(1)
            expand(2, 0, mu)
            q_full(6)
            expand(3, 0, mu)
            x_low(1)
            q_full(7)
            dve.wait_ge(qr_ready, B * DC)
            dve.wait_ge(q2_ready, B * DC)
            dve.wait_ge(q3_ready, B * DC)

            def hidden(m, b, rows, first=False):
                n = 2 * m + b
                dve.wait_ge(sig_ready, n + 1)
                nc.vector.scalar_tensor_tensor(out=gated[0:rows, b, :], in0=ps[0:rows, 2 * b, :], scalar=HS / (XS * XS),
                                               in1=sig[0:rows, b, :], op0=ALU.mult, op1=ALU.mult).then_inc(gated_ready, 1)
                dve.wait_ge(gated_ready, n + 1)
                dve.wait_ge(up_ready, n + 1)
                if not first:
                    dve.wait_ge(hlo_ready, n - 1)
                nc.vector.tensor_tensor(hid[0:rows, b, :], ps[0:rows, 2 * b + 1, :], gated[0:rows, b, :],
                                        ALU.mult).then_inc(hid_ready, 1)

            for b in range(B):
                hidden(0, b, P, first=True)
            ternary(2)
            for c in range(DC):
                expand(c, 1, md)
            with dve.Fori(1, MF - 1) as m:
                for b in range(B):
                    hidden(m, b, P)
            for b in range(B):
                hidden(MF - 1, b, FL)

            for m in range(1, MF, 2):
                dve.wait_ge(mdt_ready, m + 1)
                nc.vector.tensor_copy(mdT[:, m, :], ps[:, 4 + m % 4, 0:D // 2].bitcast(FP16)).then_inc(mdT_ready[1], 1)

            dve.wait_ge(xb_ready, 1)

            def add_down(tile):
                dve.wait_ge(down_ready, tile + 1)
                nc.vector.scalar_tensor_tensor(out=x_sb[:, tile, :], in0=ps[:, 6 + tile % 2, :], scalar=fscale[:, 0:1],
                                               in1=x_sb[:, tile, :], op0=ALU.mult, op1=ALU.add).then_inc(down_used, 1)

            def add_output(t):
                dve.wait_ge(o_ready, t + 1)
                nc.vector.tensor_tensor(x_sb[:, t, :], ps[:, 2 + t % 2, :], x_sb[:, t, :], ALU.add).then_inc(y_ready, 1)

            def combine(i, o, u):
                g, t = group(i, o), slice(2 * u, 2 * u + 2)
                dve.wait_ge(sums_ready[u], g + 1)
                sums = ps[:, 6 + u, :].rearrange("p (s e) -> p s e", e=SW)
                nc.vector.reciprocal(rden[:, t].rearrange("p t h -> p (t h)"), sums[:, :, VW - 1]).then_inc(rden_ready, 1)
                nc.vector.tensor_reduce(osum[:, t].rearrange("p t h d -> p (t h) d"),
                                        sums[:, :, 0:3 * HD].rearrange("p s (r d) -> p s d r", r=3),
                                        axis=AX.X, op=ALU.add).then_inc(osum_ready[u], 1)

            def attention(i, o, u):
                g, t = group(i, o), slice(2 * u, 2 * u + 2)
                dve.wait_ge(osum_ready[u], g + 1)
                dst = attn[:, bass.ds((g // GB) * TT + 2 * u, 2), bass.ds((g % GB) * GH * HD, GH * HD)]
                nc.vector.tensor_tensor(dst.rearrange("p t (h d) -> p t h d", h=GH), osum[:, t],
                                        rden[:, t].unsqueeze(3).to_broadcast([P, 2, GH, HD]), ALU.mult).then_inc(normed[u], 1)

            def step(i, o, what):
                def maxima(n):
                    if "m" not in what:
                        return
                    g, par = group(i, o + 3), (o + 3) % 2
                    t, heads, per = UNITS[n]
                    keys = (t + 1) * P
                    banks = slice(2 * (n % 2), 2 * (n % 2) + len(heads) // per)
                    dve.wait_ge(rows_ready, NU * g + n + 1)
                    if t < 2:
                        src = ps[:, banks, 0:per * keys].rearrange("p b (h k) -> p (b h) k", h=per)
                    else:
                        src = ps[:, banks, 0:keys]
                    nc.vector.tensor_reduce(negm[:, par, heads[0]:heads[-1] + 1, t], src, axis=AX.X, op=ALU.max,
                                            negate=True).then_inc(rows_used, 1)

                def low(n):
                    if "e" not in what:
                        return
                    e, par, s = group(i, o + 1), (o + 1) % 2, LOW_DVE[n]
                    dve.wait_ge(high_ready, NBLK * e + s + 1)
                    nc.vector.tensor_tensor(probs[:, par, s, 1, :], full[:, s, :], probs[:, par, s, 0, :],
                                            ALU.subtract).then_inc(low_ready, 1)

                def columns():
                    if "r" not in what:
                        return
                    g, par = group(i, o + 2), o % 2
                    dve.wait_ge(mt_ready, g + 1)
                    if "s" in what:
                        dve.wait_ge(mrow_st[par], 16 * (i + o // 2 + 1))
                    nc.vector.tensor_copy(mrows[:, par, :], ps[0:2 * GH * TT, MAXIMA_BANK, 0:P // 2].bitcast(BF16)).then_inc(mt_read, 1)

                for n in range(NU):
                    for s in range(UNIT_BLOCKS[n - 1] + 1 if n else 0, UNIT_BLOCKS[n] + 1):
                        if "d" in what and s in DOWN_AT:
                            add_down(DOWN_TILES * (o + 1) + DOWN_AT.index(s))
                    maxima(n)
                    if n == 0 and "p" in what:
                        combine(i, o - 1, 0)
                    if n == 1 and "p" in what:
                        attention(i, o - 1, 0)
                    if n == COPIED_AFTER:
                        columns()
                    if n in LOW_AFTER:
                        low(LOW_AFTER.index(n))
                    if n == 4 and "s" in what:
                        combine(i, o, 1)
                    if n == 5 and "s" in what:
                        attention(i, o, 1)
                if "o" in what:
                    for tile in range(OUT_TILES):
                        add_output(OUT_TILES * (o - 1) + tile)
                if "m" in what:
                    g, par = group(i, o + 3), (o + 3) % 2
                    dve.wait_ge(rows_used, NU * (g + 1))
                    if "e" in what:
                        dve.wait_ge(mt_ready, g - 1)
                    flat, shift = negm[:, par].rearrange("p h t -> p (h t)"), float(np.log(PS)) * HD ** 0.5
                    nc.vector.tensor_scalar(mparts[:, par, 0, :], flat, shift, None, ALU.add).then_inc(m1_ready, 1)
                    dve.wait_ge(m1_ready, g + 1)
                    nc.vector.scalar_tensor_tensor(out=mparts[:, par, 1, :], in0=flat, scalar=shift, in1=mparts[:, par, 0, :],
                                                   op0=ALU.add, op1=ALU.subtract).then_inc(mparts_ready, 1)

            for st in STEPS:
                if st == "loop":
                    with dve.Fori(*LOOPED) as i:
                        for o in range(2):
                            step(i, o, "mreswp")
                else:
                    step(*st)
            combine(*STEPS[-1][0:2], 0)
            attention(*STEPS[-1][0:2], 0)

            for t in range(OUT_TILES * 2, NT):
                add_output(t)

        @block.tensor
        def _(pe):
            pe.wait_ge(consts, 5)

            def transposes(n):
                pe.wait_ge(xn_ready, n + 1)
                if n >= 2:
                    pe.wait_ge(xnT_ready, n - 1)
                    pe.wait_ge(xhi_ready, n - 1)
                for c in range(DC):
                    last = nc.tensor.transpose(ps[:, n % 2, c * P:(c + 1) * P], xn[:, n % TT, c * P:(c + 1) * P], identf[:])
                last.then_inc(xt_ready, 1)

            def project_q(u):
                b, m = u // DC, u % DC
                if b:
                    pe.wait_ge(q1_ready, m + 1)
                    pe.wait_ge(qf_ready, m + 1)
                for c in range(DC):
                    last = nc.tensor.matmul(ps[:, 2 + m, :], wq_sb[:, c, m * P:(m + 1) * P], xnT[:, c, b * T:(b + 1) * T],
                                            start=c == 0, stop=c == DC - 1)
                last.then_inc(q_ready, 1)

            def project_kv(b):
                if b:
                    pe.wait_ge(kf_ready, b)
                for c in range(DC):
                    last = nc.tensor.matmul(ps[0:KV, 6, :], wkv_sb[:, c, :], xnT[:, c, b * T:(b + 1) * T],
                                            start=c == 0, stop=c == DC - 1)
                last.then_inc(k_ready, 1)

            def transpose_v(b):
                pe.wait_ge(kf_ready, b + 1)
                if b:
                    pe.wait_ge(vsb_ready, b)
                else:
                    pe.wait_ge(total_read, 1)
                for i in range(TT):
                    last = nc.tensor.transpose(ps[:, 7, i * HD:(i + 1) * HD], kvf[BANDS:KV, i * P:(i + 1) * P],
                                               identf[BANDS:KV, BANDS:KV])
                last.then_inc(v_ready, 1)

            for n in range(TT):
                transposes(n)
            pe.wait_ge(xnT_ready, TT)
            pe.wait_ge(wq_ld, 16)
            project_q(0)
            for n in range(TT, NT):
                transposes(n)
            pe.wait_ge(wsum_ready, 3)
            nc.tensor.matmul(ps[:, 7, 0:3], ones[:], wsum[:], start=True, stop=True).then_inc(total_ready, 1)
            project_q(1)
            pe.wait_ge(wkv_ld, 16)
            project_kv(0)
            project_q(2)
            transpose_v(0)
            project_q(3)
            pe.wait_ge(xnT_ready, NT)
            project_kv(1)
            project_q(4)
            transpose_v(1)
            for u in range(5, B * DC):
                project_q(u)


            def hidden(m, b, rows, first=False):
                n = 2 * m + b
                t = slice(b * T, (b + 1) * T)
                if first:
                    pe.wait_ge(xlo_ready, b + 1)
                    pe.wait_ge(q1_ready, DC + 2 * b)
                    pe.wait_ge(qf_ready, DC + 2 * b)
                else:
                    pe.wait_ge(hid_ready, n - 1)
                for w, bank, ready in ((mg, 2 * b, gate_ready), (mu, 2 * b + 1, up_ready)):
                    if first:
                        pe.wait_ge(built, DC * (bank % 2 + 1))
                    for c in range(DC):
                        for h, xh in enumerate((xhi, xlo)):
                            last = nc.tensor.matmul(ps[0:rows, bank, :], w[:, c, bass.ds(m * P, rows)], xh[:, c, t],
                                                    start=c == 0 and h == 0, stop=c == DC - 1 and h == 1)
                    last.then_inc(ready, 1)

            for b in range(B):
                hidden(0, b, P, first=True)
            with pe.Fori(1, MF - 1) as m:
                for b in range(B):
                    hidden(m, b, P)
            for b in range(B):
                hidden(MF - 1, b, FL)

            pe.wait_ge(built, DC * 3)
            pe.wait_ge(q1_ready, B * DC)
            pe.wait_ge(qf_ready, B * DC)
            pe.wait_ge(kf_ready, B)
            pe.wait_ge(vsb_ready, B)
            for m in range(MF):
                rows = P if m < MF - 1 else FL
                if m >= 4:
                    pe.wait_ge(mdT_ready[m % 2], (m - 4) // 2 + 1)
                for c in range(DC):
                    last = nc.tensor.transpose(ps[0:rows, 4 + m % 4, c * P // 2:(c + 1) * P // 2].bitcast(FP16),
                                               md[:, c, m * P:m * P + rows], ident16[:])
                last.then_inc(mdt_ready, 1)

            pe.wait_ge(mdT_ready[0], -(-MF // 2))
            pe.wait_ge(mdT_ready[1], MF // 2)
            pe.wait_ge(hlo_ready, 2 * MF)
            pe.wait_ge(hhi_ready, 2 * MF)

            def down(tile):
                if tile >= 2:
                    pe.wait_ge(down_used, tile - 1)
                for m in range(MF):
                    rows = P if m < MF - 1 else FL
                    for h in range(2):
                        last = nc.tensor.matmul(ps[:, 6 + tile % 2, :], hbuf[0:rows, h, m, tile * P:(tile + 1) * P], mdT[0:rows, m, :],
                                                start=m == 0 and h == 0, stop=m == MF - 1 and h == 1)
                last.then_inc(down_ready, 1)

            pe.wait_ge(kstack_ready, B)

            def attention_transposes(t):
                if t >= 2:
                    pe.wait_ge(attnT_ready, t - 1)
                for c in range(DC):
                    last = nc.tensor.transpose(ps[:, t % 2, c * P:(c + 1) * P], attn[:, t, c * P:(c + 1) * P], identf[:])
                last.then_inc(at_ready, 1)

            def project_out(t, chunks=range(DC)):
                if chunks[0] == 0:
                    pe.wait_ge(attnT_ready, t + 1)
                    if t >= 2:
                        pe.wait_ge(y_ready, t - 1)
                for c in chunks:
                    last = nc.tensor.matmul(ps[:, 2 + t % 2, :], attnT[:, t % 2, c, :], wo_sb[:, c, :],
                                            start=c == 0, stop=c == DC - 1, skip_group_check=True)
                if chunks[-1] == DC - 1:
                    last.then_inc(o_ready, 1)

            def step(i, o, what):
                for s, (kc, t) in enumerate(BLOCKS):
                    if "d" in what and s in DOWN_AT:
                        down(DOWN_TILES * (o + 1) + DOWN_AT.index(s))
                    if "o" in what and s in TRANSPOSED_AT:
                        tile = OUT_TILES * (o - 1) + TRANSPOSED_AT.index(s)
                        if tile == 0:
                            pe.wait_ge(rows_used, NU * NG)
                            pe.wait_ge(normed[0], GB)
                            pe.wait_ge(normed[1], GB)
                        attention_transposes(tile)
                    for k, c in OUT_AT.get(s, []) if "o" in what else []:
                        tile = OUT_TILES * (o - 1) + k
                        if tile == 0 and c == 0:
                            pe.wait_ge(wo_ld, 16)
                        if tile == 1 and c == 0:
                            pe.wait_ge(mt_read, NG)
                        project_out(tile, [c])
                    if "m" in what and s in UNIT_AT:
                        g, n = group(i, o + 3), UNIT_AT[s]
                        if s == 0:
                            pe.wait_ge(stack_ld[(o + 3) % 2], 16 * len(PAIRS) * (i + (o + 3) // 2 + 1))
                        if "r" in what or n >= 2:
                            pe.wait_ge(rows_used, NU * g + n - 1)
                        if "r" in what and n == 3:
                            pe.wait_ge(mt_read, g)
                        ut, heads, per = UNITS[n]
                        keys = (ut + 1) * P
                        for at in range(len(heads) // per):
                            bank = 2 * (n % 2) + at
                            diag = ps[:, bank, 0:per * keys].rearrange("p (h k) -> p h k", h=per)[:, :, keys - P:keys]
                            nc.tensor.matmul(diag, identb[:], maskq[:].unsqueeze(1).to_broadcast([P, per, P]),
                                             start=True, stop=False, skip_group_check=True)
                            for a in range(per):
                                h = heads[at * per + a]
                                last = nc.tensor.matmul(
                                    ps[:, bank, a * keys:(a + 1) * keys],
                                    qstack[0:BANDS, bass.ds((g % SLOTS) * GW + h * T + ut * P, P)],
                                    kstack[0:BANDS, bass.ds((g // GB) * T, keys)],
                                    start=False, stop=a == per - 1, skip_group_check=True)
                        last.then_inc(rows_ready, 1)
                    if "r" in what and s == MAXIMA_AT:
                        g, par = group(i, o + 2), o % 2
                        pe.wait_ge(mparts_ready, g + 1)
                        if "m" not in what:
                            pe.wait_ge(rows_used, NU * NG)
                        nc.tensor.transpose(ps[0:2 * GH * TT, MAXIMA_BANK, 0:P // 2].bitcast(BF16),
                                            mparts[:, par].rearrange("p a s -> p (a s)"), identb[:]).then_inc(mt_ready, 1)
                    if "e" in what:
                        g = group(i, o + 1)
                        if s == 0:
                            pe.wait_ge(mrow_ld[(o + 1) % 2], 16 * (i + (o + 1) // 2 + 1))
                        if "s" in what or s >= 2:
                            pe.wait_ge(exp_ready, NBLK * g + s - 1)
                        qs = qstack[:, bass.ds((g % SLOTS) * GW, GW)].rearrange("r (h q) -> r h q", h=GH)
                        cols = ps[:, 4 + s % 2, :].rearrange("p (h q) -> p h q", h=GH)
                        if kc == t:
                            nc.tensor.matmul(cols, identb[:], maskk[:].unsqueeze(1).to_broadcast([P, GH, P]),
                                             start=True, stop=False)
                        nc.tensor.matmul(cols, kstack[:, bass.ds((g // GB) * T + kc * P, P)], qs[:, :, t * P:(t + 1) * P],
                                         start=kc != t, stop=True).then_inc(cols_ready, 1)
                    if "s" in what:
                        g, par = group(i, o), o % 2
                        if s == FIRST_SUMS and "w" not in what:
                            pe.wait_ge(down_used, NT)
                        if s == FIRST_SUMS and "w" in what:
                            pe.wait_ge(normed[1], g)
                        for bound, upto in ((FIRST_SUMS, LAST_BLOCK[2]), (FIRST_TILE_3, NBLK - 1)):
                            if s == bound:
                                pe.wait_ge(low_ready, len(LOW_DVE) * g + sum(b <= upto for b in LOW_DVE))
                                pe.wait_ge(plow_ready, len(LOW_POOL) * g + sum(b <= upto for b in LOW_POOL))
                                pe.wait_ge(high_ready, NBLK * g + upto + 1)
                        if s == FIRST_LOW_TILES and "w" in what:
                            pe.wait_ge(normed[0], g)
                        for qt, h in SUMS_AT[s]:
                            for kt in range(qt + 1):
                                for a in range(2):
                                    last = nc.tensor.matmul(
                                        ps[:, 6 + qt // 2, ((qt % 2) * GH + h) * SW:((qt % 2) * GH + h) * SW + VW],
                                        probs[:, par, BLOCKS.index((kt, qt)), a, h * P:(h + 1) * P],
                                        v_sb[:, bass.ds((g // GB) * TT + kt, 1), :].squeeze(1),
                                        start=kt == 0 and a == 0, stop=kt == qt and a == 1)
                            if (qt, h) in LAST_SUMS:
                                last.then_inc(sums_ready[qt // 2], 1)

            for st in STEPS:
                if st == "loop":
                    with pe.Fori(*LOOPED) as i:
                        for o in range(2):
                            step(i, o, "mreswp")
                else:
                    step(*st)

            pe.wait_ge(normed[0], NG)
            pe.wait_ge(normed[1], NG)
            attention_transposes(TT)
            for t in range(TT, NT):
                if t + 1 < NT:
                    attention_transposes(t + 1)
                project_out(t)


def octonion_signs():
    s = np.zeros((J, J, J), np.float32)
    s[0, 0, 0] = 1.0
    for i in range(1, J):
        s[0, i, i] = s[i, 0, i] = 1.0
        s[i, i, 0] = -1.0
    for a, b, c in [(1, 2, 3), (1, 4, 5), (1, 7, 6), (2, 4, 6), (2, 5, 7), (3, 4, 7), (3, 6, 5)]:
        for p, q, r in ((a, b, c), (b, c, a), (c, a, b)):
            s[p, q, r], s[q, p, r] = 1.0, -1.0
    return s


def slots(w, component_last):
    w = w.transpose(0, 2, 1) if component_last else w
    halves = [w[[j ^ h for j in range(J)]].transpose(1, 0, 2).reshape(OD, F) for h in range(2)]
    return np.ascontiguousarray(np.concatenate(halves, 0))


def kernel(**inputs):
    import concourse.bacc as bacc
    from concourse.bass_utils import run_bass_kernel_spmd

    a = {k.replace("L0_", ""): np.asarray(v) for k, v in inputs.items()}
    s = octonion_signs()
    signs = np.zeros((P, 2, DC, J), np.float32)
    for c in range(DC):
        for h in range(2):
            for k in range(J):
                rows = slice(h * OD, (h + 1) * OD)
                i = 2 * c + h
                signs[rows, 0, c, k] = s[i ^ k, i, k]
                signs[rows, 1, c, k] = s[i ^ k, k, i]
    bands = np.zeros((BANDS, 3), np.float32)
    for r, (_, part) in enumerate(PAIRS):
        bands[r * HD:(r + 1) * HD, part] = 1.0
    arrays = {
        "x": a["attn_x"].reshape(TOK, D),
        "wqT": a["attn_wq_w"].T,
        "wkvT": np.concatenate([a["attn_wk_w"].T] * len(PAIRS) + [a["attn_wv_w"].T], 1),
        "woT": a["attn_wo_w"].T,
        "bq": a["attn_wq_b"].reshape(DC, P).T,
        "bkv": np.concatenate([a["attn_wk_b"]] * len(PAIRS) + [a["attn_wv_b"]]).reshape(KV, 1),
        "bo": a["attn_wo_b"],
        "wg": slots(a["ffn_w_gate"], True),
        "wu": slots(a["ffn_w_up"], True),
        "wd": slots(a["ffn_w_down"], False),
        "signs": signs.reshape(P, 2 * DC * J),
        "bands": bands,
    }
    arrays = {k: np.ascontiguousarray(v) for k, v in arrays.items()}
    nc = bacc.Bacc("TRN2", target_bir_lowering=False, num_devices=1)
    args = [nc.dram_tensor(k, v.shape, mybir.dt.from_np(v.dtype), kind="ExternalInput").ap() for k, v in arrays.items()]
    out = nc.dram_tensor("out", (TOK, D), FP32, kind="ExternalOutput").ap()
    build(nc, *args, out)
    r = run_bass_kernel_spmd(nc, [arrays], core_ids=[0])
    return r.results[0]["out"].reshape(a["attn_x"].shape)
```

```python
import numpy as np
import concourse.bass as bass
from concourse import mybir
from contextlib import ExitStack

FP32 = mybir.dt.float32
BF16 = mybir.dt.bfloat16
FP16 = mybir.dt.float16
ALU = mybir.AluOpType
ACT = mybir.ActivationFunctionType
AX = mybir.AxisListType

P = 128
B, T, D = 2, 512, 512
TOK = B * T
NT = TOK // P
TT = T // P
DC = D // P
H, HD = 32, 16
VW = 1 + 3 * HD
VL = 1 + 2 * HD
SW = 64
J, OD, HID = 8, D // 8, 170
F = J * HID
MF = -(-F // P)
FL = F - (MF - 1) * P
GH = 4
NG = B * H // GH
GB = NG // B
GW = GH * T
PAIRS = [(0, 0), (0, 1), (0, 2), (1, 0), (1, 1), (2, 0)]
BANDS = len(PAIRS) * HD
ROWS = BANDS + 2
KV = BANDS + HD
QSLOTS = 4
SLOTS = 4
BLOCKS = [(kc, t) for t in range(TT) for kc in range(t + 1)]
NBLK = len(BLOCKS)
UNITS = [(1, (0, 1, 2, 3), 2), (0, (0, 1, 2, 3), 4), (2, (0, 1), 1), (2, (2, 3), 1), (3, (0, 1), 1), (3, (2, 3), 1)]
NU = len(UNITS)
UNIT_AT = {0: 0, 2: 1, 3: 2, 5: 3, 7: 4, 9: 5}
DOWN_BANK = 7
DOWN_WHOLE = {3: (0, 2), 4: (2, 3), 5: (3, 5), 6: (5, 6), 7: (6, 8), 8: (8, 9), 9: (9, MF)}
DOWN_HALF = [{1: (0, 1), 2: (1, 2), 3: (2, 3), 7: (3, 5), 8: (5, 6)},
             {1: (6, 7), 2: (7, 8), 3: (8, 9), 7: (9, 10), 8: (10, MF)}]
TRANSPOSED_AT = {1: {1: 0, 6: 1}, 2: {2: 2, 7: 3}, 3: {}}
COPIED_AT = {1: {2: 0, 8: 1}, 2: {4: 2, 9: 3}, 3: {}}
OUT_AT = {1: {4: [(0, 0)], 5: [(0, 1)], 6: [(0, 2)], 7: [(0, 3)]},
          2: {1: [(1, 0)], 2: [(1, 1)], 3: [(1, 2)], 4: [(1, 3)], 5: [(2, 0)], 6: [(2, 1)], 7: [(2, 2)], 8: [(2, 3)]},
          3: {1: [(3, 0), (3, 1)], 7: [(3, 2), (3, 3)]}}
ADDED_AT = {1: {5: 0}, 2: {3: 1, 5: 2}, 3: {5: 3}}
HELD = 5
SUMS_AT = [[], [], [], [(2, 0), (2, 1)], [(2, 2), (2, 3)], [(3, 0), (3, 1), (3, 2), (3, 3)], [], [], [],
           [(1, 0), (1, 1), (1, 2), (1, 3), (0, 0), (0, 1), (0, 2), (0, 3)]]
FIRST_SUMS, FIRST_TILE_3, FIRST_LOW_TILES = (min(s for s, sums in enumerate(SUMS_AT) if any(t in tiles for t, _ in sums))
                                             for tiles in ((0, 1, 2, 3), (3,), (0, 1)))
LAST_SUMS = [[(t, h) for sums in SUMS_AT for t, h in sums if t // 2 == u][-1] for u in range(2)]
LAST_BLOCK = [max(s for s, (_, u) in enumerate(BLOCKS) if u == t) for t in range(TT)]
MAXIMA_AT = 2
MAXIMA_BANK = 3
COPIED_AFTER = 1
LOW_DVE = (5,)
LOW_AFTER = (4,)
LOW_POOL = [s for s in range(NBLK) if s not in LOW_DVE]
TILE_SETS = (slice(0, 2), slice(2, TT), slice(TT, NT))
EPS = 1e-5
WARM_UPS = 19
XS = 1024.0
HS = 0.125
PS = 1024.0
MASKED = -1e30


def build(nc, x, wqT, wkvT, woT, bq, bkv, bo, wg, wu, wd, signs, bands, out):
    ctx = ExitStack()
    with ctx:
        def sb(name, shape, dt=FP32):
            return ctx.enter_context(nc.sbuf_tensor(name, shape, dt))

        def sem(name):
            return ctx.enter_context(nc.semaphore(name))

        x_sb = sb("x_sb", [P, NT, D])
        work = sb("work", [P, 2, TT, D])
        xn, wq_sb = work[:, 0], work[:, 1]
        flat_work = work[:].rearrange("p a t n -> p (a t n)")
        attnT = flat_work[:, 0:2 * D].rearrange("p (s c q) -> p s c q", s=2, c=DC)
        full = flat_work[:, 2 * D:(2 + HELD) * D].rearrange("p (s n) -> p s n", s=HELD)
        xnT = sb("xnT", [P, DC, TOK])
        attn = xnT[:].rearrange("p c t -> p (c t)").rearrange("p (g t n) -> p g t n", g=NG // 2, t=TT)
        mdT = sb("mdT", [P, MF, D], FP16)
        xhl = sb("xhl", [P, 2, DC, TOK], FP16)
        xhi, xlo = xhl[:, 0], xhl[:, 1]
        wkv_sb = sb("wkv_sb", [P, DC, KV])
        wo_sb = sb("wo_sb", [P, DC, D])
        bq_sb = sb("bq_sb", [P, DC])
        bkv_sb = sb("bkv_sb", [KV, 1])
        bo_sb = sb("bo_sb", [P, D])
        signs_sb = sb("signs_sb", [P, 2, DC, J])
        bands_sb = sb("bands_sb", [BANDS, 3])
        raw = sb("raw", [P, max(3 * F, SLOTS * GW // 2)])
        qstack = raw[0:ROWS, 0:SLOTS * GW // 2].bitcast(BF16)
        neg = sb("neg", [P, F], FP16)
        tern = sb("tern", [P, F], FP16)
        mgu = sb("mgu", [P, 2, DC, F], FP16)
        mg, mu = mgu[:, 0], mgu[:, 1]
        md = sb("md", [P, DC, F], FP16)
        pairs = mgu[:].rearrange("p w c f -> p (w c f)")[:, 0:2 * NBLK * GH * P].rearrange("p (a s n) -> p a s n", a=2, s=NBLK)
        highs = md[:].rearrange("p c f -> p (c f)")[:, 0:NBLK * GH * P].rearrange("p (s n) -> p s n", s=NBLK)
        lows = xhl[:].rearrange("p a c t -> p (a c t)")[:, 0:NBLK * GH * P].rearrange("p (s n) -> p s n", s=NBLK)
        probs = [[pairs[:, 0], pairs[:, 1]], [highs, lows]]
        hbuf = sb("hbuf", [P, 2, MF, TOK], FP16)
        zeros = hbuf[:, 0, 0, 0:T]
        under = hbuf[:, 1].rearrange("p m t -> p (m t)").bitcast(BF16)
        qpart = under[:, 0:12 * T].rearrange("p (r s t) -> p r s t", r=3, s=QSLOTS)
        kpart = under[0:BANDS, 12 * T:15 * T].rearrange("p (r t) -> p r t", r=3)
        kband = under[0:BANDS, 15 * T:18 * T].rearrange("p (r t) -> p r t", r=3)
        kstack = sb("kstack", [ROWS, TOK], BF16)
        v_sb = sb("v_sb", [P, NT, VW], BF16)
        vf = sb("vf", [P, TT, HD])
        vr = sb("vr", [P, TT, HD])
        osum = sb("osum", [P, TT, GH, HD])
        sig = sb("sig", [P, 2, T])
        gated = sb("gated", [P, 2, T])
        hid = sb("hid", [P, 2, T])
        kvf = sig[0:KV, 0, :]
        kf, kr = sig[0:BANDS, 0, :], sig[0:BANDS, 1, :]
        qf, qr = gated, hid
        stats = sb("stats", [P, NT, 6])
        mv = sb("mv", [P, NT, 2])
        vare = sb("vare", [P, NT])
        half = sb("half", [P, NT])
        rstd = sb("rstd", [P, NT])
        wsum = sb("wsum", [P, 3])
        scale = sb("scale", [P, 3])
        thr = sb("thr", [P, 3])
        nthr = sb("nthr", [P, 3])
        gscale = sb("gscale", [P, 1])
        fprod = sb("fprod", [P, 1])
        fscale = sb("fscale", [P, 1])
        ones = sb("ones", [P, P])
        identf = sb("identf", [P, P])
        ident16 = sb("ident16", [P, P], FP16)
        identb = sb("identb", [P, P], BF16)
        maskq = sb("maskq", [P, P], BF16)
        maskk = sb("maskk", [P, P], BF16)
        negm = sb("negm", [P, 2, GH, TT])
        mparts = sb("mparts", [P, 2, 2, GH * TT], BF16)
        mrows = sb("mrows", [2 * GH * TT, 2, P], BF16)
        rden = sb("rden", [P, TT, GH])
        ps = ctx.enter_context(nc.psum_tensor("ps", [P, 8, 512], FP32))
        q_dram = nc.dram_tensor("q_parts", [3, D, TOK], BF16, kind="Internal").ap()

        m_dram = nc.dram_tensor("minus_maxima", [NG, 2 * GH * TT, P], BF16, kind="Internal").ap()

        x_ld = [sem(f"x_ld{i}") for i in range(NT // 2)]
        wq_ld, wkv_ld, wo_ld, small_ld = sem("wq_ld"), sem("wkv_ld"), sem("wo_ld"), sem("small_ld")
        raw_ld = [sem(f"raw_ld{i}") for i in range(3)]
        filled, consts, zeros_ready = sem("filled"), sem("consts"), sem("zeros_ready")
        stats_done, mv_done, vare_ready, rstd_ready = sem("stats_done"), sem("mv_done"), sem("vare_ready"), sem("rstd_ready")
        xn_ready, xt_ready, xnT_ready, xhi_ready, xlo_ready = (sem("xn_ready"), sem("xt_ready"), sem("xnT_ready"),
                                                               sem("xhi_ready"), sem("xlo_ready"))
        xb_ready = sem("xb_ready")
        q_ready, q1_ready, qf_ready, qr_ready, q2_ready, q3_ready = (sem("q_ready"), sem("q1_ready"), sem("qf_ready"),
                                                                     sem("qr_ready"), sem("q2_ready"), sem("q3_ready"))
        q_out = [sem(f"q_out{i}") for i in range(QSLOTS)]
        k_ready, kf_ready, k1_ready, kr_ready, k2_ready, k3_ready = (sem("k_ready"), sem("kf_ready"), sem("k1_ready"),
                                                                     sem("kr_ready"), sem("k2_ready"), sem("k3_ready"))
        kband_ready, ksum_ready, kstack_ready = sem("kband_ready"), sem("ksum_ready"), sem("kstack_ready")
        v_ready, vsb_ready = sem("v_ready"), sem("vsb_ready")
        wsum_ready, total_ready, total_read, schain, scales_ready = (sem("wsum_ready"), sem("total_ready"), sem("total_read"),
                                                                     sem("schain"), sem("scales_ready"))
        neg_done, tern_done, built = sem("neg_done"), sem("tern_done"), sem("built")
        gate_ready, up_ready, sig_ready, gated_ready = sem("gate_ready"), sem("up_ready"), sem("sig_ready"), sem("gated_ready")
        hid_ready, hhi_ready, hlo_ready = sem("hid_ready"), sem("hhi_ready"), sem("hlo_ready")
        mdt_ready, down_ready, down_used = sem("mdt_ready"), sem("down_ready"), sem("down_used")
        mdT_ready = [sem("mdT_ready_act"), sem("mdT_ready_dve")]
        stack_ld = [sem("stack_ld0"), sem("stack_ld1")]
        mrow_st = [sem("mrow_st0"), sem("mrow_st1")]
        mrow_ld = [sem("mrow_ld0"), sem("mrow_ld1")]
        rows_ready, rows_used, m1_ready, mparts_ready = sem("rows_ready"), sem("rows_used"), sem("m1_ready"), sem("mparts_ready")
        mt_ready, mt_read, cols_ready, exp_ready = sem("mt_ready"), sem("mt_read"), sem("cols_ready"), sem("exp_ready")
        high_ready, low_ready, plow_ready = sem("high_ready"), sem("low_ready"), sem("plow_ready")
        vchain = sem("vchain")
        rden_ready = sem("rden_ready")
        sums_ready, osum_ready, normed = ([sem(f"{name}{u}") for u in range(2)] for name in ("sums_ready", "osum_ready", "normed"))
        at_ready, attnT_ready, o_ready, y_ready, y_out = (sem("at_ready"), sem("attnT_ready"), sem("o_ready"), sem("y_ready"),
                                                          sem("y_out"))

        block = ctx.enter_context(nc.Block())

        STEPS = [(-1, -1, "mD"), (-1, 0, "mrD"), (-1, 1, "mreD"), (0, 0, "mres"), (0, 1, "mreswp"), "loop",
                 (6, 0, "mreswp"), (6, 1, "reswpo"), (6, 2, "eswpo"), (6, 3, "swpo")]
        LOOPED = (1, 6)

        def group(i, o):
            return 2 * i + o

        @block.sync
        def _(sp):
            x_t = x.rearrange("(n p) d -> p n d", p=P)
            for i in range(NT // 2):
                sp.dma_start(x_sb[:, 2 * i:2 * i + 2, :], x_t[:, 2 * i:2 * i + 2, :]).then_inc(x_ld[i], 16)
            sp.dma_start(wq_sb[:], wqT.rearrange("(c p) n -> p c n", p=P)).then_inc(wq_ld, 16)
            for i, w in enumerate((wg, wu, wd)):
                sp.dma_start(raw[:, i * F:(i + 1) * F], w).then_inc(raw_ld[i], 16)
            sp.dma_start(wo_sb[:], woT.rearrange("(c p) n -> p c n", p=P)).then_inc(wo_ld, 16)
            for u in range(B * DC):
                b, m, s = u // DC, u % DC, u % QSLOTS
                sp.wait_ge(q1_ready, u + 1)
                sp.wait_ge(q2_ready, u + 1)
                sp.wait_ge(q3_ready, u + 1)
                sp.dma_start(q_dram[:, m * P:(m + 1) * P, b * T:(b + 1) * T].rearrange("r p t -> p r t"),
                             qpart[:, :, s, :]).then_inc(q_out[s], 16)

            def load_stack(i, o):
                g = group(i, o)
                for r, (part, _) in enumerate(PAIRS):
                    sp.dma_start(
                        qstack[r * HD:(r + 1) * HD, bass.ds((g % SLOTS) * GW, GW)].rearrange("d (h t) -> d h t", h=GH),
                        q_dram[part, bass.ds((g % GB) * GH * HD, GH * HD), bass.ds((g // GB) * T, T)]
                        .rearrange("(h d) t -> d h t", d=HD)).then_inc(stack_ld[o % 2], 16)

            def load_maxima(i, o):
                g = group(i, o)
                sp.wait_ge(mt_read, g + 1)
                sp.dma_start(m_dram[bass.ds(g, 1)].squeeze(0), mrows[:, o % 2, :]).then_inc(mrow_st[o % 2], 16)
                sp.wait_ge(mrow_st[o % 2], 16 * (i + o // 2 + 1))
                sp.dma_start(qstack[BANDS:ROWS, bass.ds((g % SLOTS) * GW, GW)],
                             m_dram[bass.ds(g, 1)].squeeze(0).rearrange("(r s) q -> r (s q)", r=2)).then_inc(mrow_ld[o % 2], 16)

            for s in range(QSLOTS):
                sp.wait_ge(q_out[s], 16 * B * DC // QSLOTS)
            sp.wait_ge(tern_done, 3)
            load_stack(0, 0)
            load_stack(0, 1)
            sp.wait_ge(stack_ld[0], 16 * len(PAIRS))
            load_stack(0, 2)
            sp.wait_ge(stack_ld[1], 16 * len(PAIRS))
            load_stack(0, 3)

            def step(i, o, what, stack):
                if stack:
                    sp.wait_ge(cols_ready, NBLK * (group(i, o) + 1))
                    load_stack(i, o + 4)
                if "r" in what:
                    load_maxima(i, o + 2)

            for st in STEPS:
                if st == "loop":
                    with sp.Fori(*LOOPED) as i:
                        for o in range(2):
                            step(i, o, "mreswpd", True)
                else:
                    step(*st, st[0] == 0)

            out_t = out.rearrange("(n p) d -> p n d", p=P)
            for t in range(NT):
                sp.wait_ge(y_ready, t + 1)
                sp.dma_start(out_t[:, t, :], x_sb[:, t, :]).then_inc(y_out, 16)
            sp.wait_ge(y_out, 16 * NT)

        @block.gpsimd
        def _(pool):
            for m in (identf, ident16, identb, maskq, maskk):
                nc.gpsimd.memset(m[:], 0.0).then_inc(filled, 1)
            nc.gpsimd.memset(ones[:], 1.0).then_inc(filled, 1)
            nc.gpsimd.memset(half[:], -0.5).then_inc(filled, 1)
            nc.gpsimd.memset(v_sb[:, :, 0:1], 1.0).then_inc(filled, 1)
            pool.wait_ge(filled, 8)
            nc.gpsimd.memset(kstack[BANDS:ROWS, :], 1.0).then_inc(filled, 1)
            pool.wait_ge(filled, 9)
            for m in (identf, ident16, identb):
                nc.gpsimd.affine_select(out=m[:], in_=m[:], compare_op=ALU.not_equal, fill=1.0, base=0,
                                        pattern=[[-1, P]], channel_multiplier=1).then_inc(consts, 1)
            nc.gpsimd.affine_select(out=maskq[:], in_=maskq[:], compare_op=ALU.is_ge, fill=MASKED, base=0,
                                    pattern=[[-1, P]], channel_multiplier=1).then_inc(consts, 1)
            nc.gpsimd.affine_select(out=maskk[:], in_=maskk[:], compare_op=ALU.is_ge, fill=MASKED, base=0,
                                    pattern=[[1, P]], channel_multiplier=-1).then_inc(consts, 1)

            def rsqrt(t):
                pool.wait_ge(vare_ready, t.stop)
                nc.gpsimd.tensor_tensor(rstd[:, t], vare[:, t], half[:, t], ALU.pow).then_inc(rstd_ready, t.stop - t.start)

            def q_rest(u):
                s = u % 2
                pool.wait_ge(qf_ready, u + 1)
                pool.wait_ge(q1_ready, u + 1)
                if u >= 2:
                    pool.wait_ge(q2_ready, u - 1)
                    pool.wait_ge(q3_ready, u - 1)
                nc.gpsimd.tensor_tensor(qr[:, s, :], qf[:, s, :], qpart[:, 0, u % QSLOTS, :], ALU.subtract).then_inc(qr_ready, 1)

            def q_third(u):
                pool.wait_ge(qr_ready, u + 1)
                pool.wait_ge(q2_ready, u + 1)
                nc.gpsimd.tensor_tensor(qpart[:, 2, u % QSLOTS, :], qr[:, u % 2, :], qpart[:, 1, u % QSLOTS, :],
                                        ALU.subtract).then_inc(q3_ready, 1)

            def k_rest(b):
                pool.wait_ge(k1_ready, b + 1)
                nc.gpsimd.tensor_tensor(kr, kf, kpart[:, 0, :], ALU.subtract).then_inc(kr_ready, 1)

            def k_third(b):
                pool.wait_ge(kr_ready, b + 1)
                pool.wait_ge(k2_ready, b + 1)
                nc.gpsimd.tensor_tensor(kpart[:, 2, :], kr, kpart[:, 1, :], ALU.subtract).then_inc(k3_ready, 1)

            def k_bands(b):
                pool.wait_ge(kband_ready, 3 * (b + 1))
                nc.gpsimd.tensor_tensor(kband[:, 0, :], kband[:, 0, :], kband[:, 1, :], ALU.add).then_inc(ksum_ready, 1)
                pool.wait_ge(ksum_ready, b + 1)
                nc.gpsimd.tensor_tensor(kstack[0:BANDS, b * T:(b + 1) * T], kband[:, 0, :], kband[:, 2, :],
                                        ALU.add).then_inc(kstack_ready, 1)

            for t in TILE_SETS:
                rsqrt(t)
            q_rest(0)
            q_rest(1)
            q_third(0)
            k_rest(0)
            q_third(1)
            q_rest(2)
            k_third(0)
            q_rest(3)
            q_third(2)
            k_bands(0)
            k_rest(1)
            q_third(3)
            q_rest(4)
            k_third(1)
            q_rest(5)
            q_third(4)
            for u in range(6, B * DC):
                q_rest(u)
                q_third(u - 1)
            q_third(B * DC - 1)
            k_bands(1)
            pool.wait_ge(small_ld, 16 * 5)

            def hidden_low(m, b, rows):
                n = 2 * m + b
                pool.wait_ge(hid_ready, n + 1)
                pool.wait_ge(hhi_ready, n + 1)
                cols = slice(b * T, (b + 1) * T)
                nc.gpsimd.tensor_tensor(hbuf[0:rows, 1, bass.ds(m, 1), cols].squeeze(1), hid[0:rows, b, :],
                                        hbuf[0:rows, 0, bass.ds(m, 1), cols].squeeze(1), ALU.subtract).then_inc(hlo_ready, 1)

            for s in range(QSLOTS):
                pool.wait_ge(q_out[s], 16 * B * DC // QSLOTS)
            pool.wait_ge(xn_ready, NT)
            with pool.Fori(0, NT) as m:
                for b in range(B):
                    hidden_low(m, b, P)
                row = x_sb[:, bass.ds(m, 1), :].squeeze(1)
                nc.gpsimd.tensor_tensor(row, row, bo_sb[:], ALU.add).then_inc(xb_ready, 1)
            with pool.Fori(NT, MF - 1) as m:
                for b in range(B):
                    hidden_low(m, b, P)
            for b in range(B):
                hidden_low(MF - 1, b, FL)

            def step(i, o, what):
                if "e" not in what:
                    return
                e, par = group(i, o + 1), (o + 1) % 2
                for s in LOW_POOL:
                    pool.wait_ge(high_ready, NBLK * e + s + 1)
                    nc.gpsimd.tensor_tensor(probs[par][1][:, s, :], full[:, s % HELD, :], probs[par][0][:, s, :],
                                            ALU.subtract).then_inc(plow_ready, 1)

            for st in STEPS:
                if st == "loop":
                    with pool.Fori(*LOOPED) as i:
                        for o in range(2):
                            step(i, o, "mreswpd")
                else:
                    step(*st)

        @block.scalar
        def _(act):
            act.dma_start(bq_sb[:], bq).then_inc(small_ld, 16)
            act.dma_start(bkv_sb[:], bkv).then_inc(small_ld, 16)
            act.dma_start(signs_sb[:].rearrange("p a c k -> p (a c k)"), signs).then_inc(small_ld, 16)
            act.dma_start(bands_sb[:], bands).then_inc(small_ld, 16)
            act.dma_start(bo_sb[:], bo.rearrange("(a n) -> a n", a=1).to_broadcast([P, D])).then_inc(small_ld, 16)
            act.dma_start(wkv_sb[:], wkvT.rearrange("(c p) n -> p c n", p=P)).then_inc(wkv_ld, 16)

            def q_first(u):
                s = u % QSLOTS
                act.wait_ge(q_ready, u + 1)
                if u >= QSLOTS:
                    act.wait_ge(q_out[s], 16 * (u // QSLOTS))
                nc.scalar.activation(qpart[:, 0, s, :], ps[:, 2 + u % DC, :], ACT.Identity,
                                     bias=bq_sb[:, u % DC:u % DC + 1]).then_inc(q1_ready, 1)

            def q_second(u):
                act.wait_ge(qr_ready, u + 1)
                nc.scalar.activation(qpart[:, 1, u % QSLOTS, :], qr[:, u % 2, :], ACT.Copy).then_inc(q2_ready, 1)

            def k_first(b):
                act.wait_ge(k_ready, b + 1)
                if b:
                    act.wait_ge(kstack_ready, b)
                    act.wait_ge(v_ready, b)
                nc.scalar.activation(kvf, ps[0:KV, 6, :], ACT.Identity, bias=bkv_sb[:, 0:1]).then_inc(kf_ready, 1)
                act.wait_ge(kf_ready, b + 1)
                nc.scalar.activation(kpart[:, 0, :], kf, ACT.Copy).then_inc(k1_ready, 1)

            def k_second(b):
                act.wait_ge(kr_ready, b + 1)
                nc.scalar.activation(kpart[:, 1, :], kr, ACT.Copy).then_inc(k2_ready, 1)

            def k_masked(b):
                act.wait_ge(k2_ready, b + 1)
                act.wait_ge(k3_ready, b + 1)
                for r in range(3):
                    nc.scalar.activation(kband[:, r, :], kpart[:, r, :], ACT.Copy,
                                         scale=bands_sb[:, r:r + 1]).then_inc(kband_ready, 1)

            def x_high(b):
                t = slice(b * T, (b + 1) * T)
                act.wait_ge(xnT_ready, (b + 1) * TT)
                for c in range(DC):
                    nc.scalar.activation(xhi[:, c, t], xnT[:, c, t], ACT.Copy, scale=XS).then_inc(xhi_ready, 1)

            for n in range(NT):
                act.wait_ge(xt_ready, n + 1)
                src = ps[:, n % 2, :].rearrange("p (c q) -> p c q", c=DC)
                nc.scalar.activation(xnT[:, :, n * P:(n + 1) * P], src, ACT.Copy).then_inc(xnT_ready, 1)
                if n == TT - 1:
                    x_high(0)
            act.wait_ge(small_ld, 16 * 5)
            q_first(0)
            q_first(1)
            q_second(0)
            k_first(0)
            q_second(1)
            x_high(1)
            q_first(2)
            k_second(0)
            q_first(3)
            q_second(2)
            k_masked(0)
            k_first(1)
            q_second(3)
            q_first(4)
            k_second(1)
            q_first(5)
            q_second(4)
            k_masked(1)
            for u in range(6, B * DC):
                q_first(u)
                q_second(u - 1)

            def sigmoid(m, b, rows):
                n = 2 * m + b
                act.wait_ge(gate_ready, n + 1)
                nc.scalar.activation(sig[0:rows, b, :], ps[0:rows, 2 * b, :], ACT.Sigmoid,
                                     scale=gscale[0:rows, 0:1]).then_inc(sig_ready, 1)

            def hidden_high(m, b, rows):
                n = 2 * m + b
                cols = slice(b * T, (b + 1) * T)
                act.wait_ge(hid_ready, n + 1)
                nc.scalar.activation(hbuf[0:rows, 0, bass.ds(m, 1), cols].squeeze(1), hid[0:rows, b, :],
                                     ACT.Copy).then_inc(hhi_ready, 1)

            act.wait_ge(kr_ready, B)
            act.wait_ge(k3_ready, B)
            act.wait_ge(v_ready, B)
            act.wait_ge(scales_ready, 1)
            sigmoid(0, 0, P)
            q_second(B * DC - 1)
            hidden_high(0, 0, P)
            sigmoid(0, 1, P)
            hidden_high(0, 1, P)
            with act.Fori(1, MF - 1) as m:
                for b in range(B):
                    sigmoid(m, b, P)
                    hidden_high(m, b, P)
            for b in range(B):
                sigmoid(MF - 1, b, FL)
                hidden_high(MF - 1, b, FL)
            for m in range(0, MF, 2):
                rows = P if m < MF - 1 else FL
                act.wait_ge(mdt_ready, m + 1)
                nc.scalar.activation(mdT[0:rows, m, :], ps[0:rows, 4 + m % 4, 0:D // 2].bitcast(FP16),
                                     ACT.Copy).then_inc(mdT_ready[0], 1)

            def copy_transposed(t):
                act.wait_ge(at_ready, t + 1)
                if t >= 2:
                    act.wait_ge(o_ready, t - 1)
                nc.scalar.activation(attnT[:, t % 2], ps[:, t % 2, :].rearrange("p (c q) -> p c q", c=DC),
                                     ACT.Copy).then_inc(attnT_ready, 1)

            def step(i, o, what):
                if "e" not in what:
                    return
                e, par = group(i, o + 1), (o + 1) % 2
                for s in range(NBLK + 1):
                    if "o" in what and s in COPIED_AT[o]:
                        copy_transposed(COPIED_AT[o][s])
                    if s < NBLK:
                        act.wait_ge(cols_ready, NBLK * e + s + 1)
                        if s == 0 and "w" in what:
                            act.wait_ge(sums_ready[0], e - 1)
                        if s >= HELD or "s" in what:
                            back, ge = (s - HELD, e) if s >= HELD else (s - HELD + NBLK, e - 1)
                            if back in LOW_DVE:
                                act.wait_ge(low_ready, len(LOW_DVE) * ge + LOW_DVE.index(back) + 1)
                            else:
                                act.wait_ge(plow_ready, len(LOW_POOL) * ge + LOW_POOL.index(back) + 1)
                        nc.scalar.activation(full[:, s % HELD, :], ps[:, 4 + s % 2, :], ACT.Exp,
                                             scale=float(HD) ** -0.5).then_inc(exp_ready, 1)
                    if s:
                        h = s - 1
                        act.wait_ge(exp_ready, NBLK * e + h + 1)
                        nc.scalar.activation(probs[par][0][:, h, :], full[:, h % HELD, :], ACT.Copy).then_inc(high_ready, 1)

            for st in STEPS:
                if st == "loop":
                    with act.Fori(*LOOPED) as i:
                        for o in range(2):
                            step(i, o, "mreswpd")
                else:
                    step(*st)

            for t in range(TT, NT):
                copy_transposed(t)

        @block.vector
        def _(dve):
            def statistics(t):
                for n in range(t.start, t.stop):
                    dve.wait_ge(x_ld[n // 2], 16)
                    nc.vector.bn_stats(stats[:, n, :], x_sb[:, n, :]).then_inc(stats_done, 1)
                for n in range(t.start, t.stop):
                    dve.wait_ge(stats_done, n + 1)
                    nc.vector.bn_aggr(mv[:, n, :], stats[:, n, :]).then_inc(mv_done, 1)
                dve.wait_ge(mv_done, t.stop)
                nc.vector.tensor_scalar(vare[:, t], mv[:, t, 1], EPS, None, ALU.add).then_inc(vare_ready, t.stop - t.start)

            def normalise(t):
                dve.wait_ge(rstd_ready, t.stop)
                for n in range(t.start, t.stop):
                    if n >= TT:
                        dve.wait_ge(xt_ready, n - TT + 1)
                    nc.vector.tensor_scalar(xn[:, n % TT, :], x_sb[:, n, :], mv[:, n, 0:1], rstd[:, n:n + 1],
                                            ALU.subtract, ALU.mult).then_inc(xn_ready, 1)

            def x_low(b):
                dve.wait_ge(xnT_ready, (b + 1) * TT)
                dve.wait_ge(xhi_ready, (b + 1) * DC)
                t = slice(b * T, (b + 1) * T)
                for c in range(DC):
                    last = nc.vector.scalar_tensor_tensor(out=xlo[:, c, t], in0=xnT[:, c, t], scalar=XS,
                                                          in1=xhi[:, c, t], op0=ALU.mult, op1=ALU.subtract)
                last.then_inc(xlo_ready, 1)

            def q_full(u):
                s = u % 2
                dve.wait_ge(q1_ready, u + 1)
                if u >= 2:
                    dve.wait_ge(qr_ready, u - 1)
                nc.vector.tensor_scalar(qf[:, s, :], ps[:, 2 + u % DC, :], bq_sb[:, u % DC:u % DC + 1], None,
                                        ALU.add).then_inc(qf_ready, 1)

            vlinks = [0]

            def vlink(ins):
                vlinks[0] += 1
                ins.then_inc(vchain, 1)
                dve.wait_ge(vchain, vlinks[0])

            def v_parts(b):
                dve.wait_ge(v_ready, b + 1)
                vp = v_sb[:, b * TT:(b + 1) * TT, 1:VW].rearrange("p t (r d) -> p r t d", r=3)
                vlink(nc.vector.tensor_copy(vf[:].rearrange("p t d -> p (t d)"), ps[:, 7, 0:TT * HD]))
                vlink(nc.vector.tensor_copy(vp[:, 0], vf[:]))
                vlink(nc.vector.tensor_tensor(vr[:], vf[:], vp[:, 0], ALU.subtract))
                vlink(nc.vector.tensor_copy(vp[:, 1], vr[:]))
                nc.vector.tensor_tensor(vp[:, 2], vr[:], vp[:, 1], ALU.subtract).then_inc(vsb_ready, 1)

            def negatives(w):
                if w:
                    dve.wait_ge(built, DC * w)
                nc.vector.tensor_scalar(neg[:], raw[:, w * F:(w + 1) * F], nthr[:, w:w + 1], None,
                                        ALU.is_lt).then_inc(neg_done, 1)

            def ternary(w):
                dve.wait_ge(neg_done, w + 1)
                nc.vector.scalar_tensor_tensor(out=tern[:], in0=raw[:, w * F:(w + 1) * F], scalar=thr[:, w:w + 1], in1=neg[:],
                                               op0=ALU.is_gt, op1=ALU.subtract).then_inc(tern_done, 1)
                dve.wait_ge(tern_done, w + 1)

            def expand(c, kind, dst):
                for k in range(J):
                    j = (2 * c) ^ k
                    last = nc.vector.tensor_scalar(dst[:, c, k * HID:(k + 1) * HID], tern[:, j * HID:(j + 1) * HID],
                                                   signs_sb[:, kind, c, k:k + 1], None, ALU.mult)
                last.then_inc(built, 1)

            nc.vector.memset(zeros, 0.0).then_inc(zeros_ready, 1)
            statistics(TILE_SETS[0])
            statistics(TILE_SETS[1])
            normalise(TILE_SETS[0])
            normalise(TILE_SETS[1])
            statistics(TILE_SETS[2])
            normalise(TILE_SETS[2])
            for w in range(3):
                dve.wait_ge(raw_ld[w], 16)
                nc.vector.tensor_reduce(wsum[:, w:w + 1], raw[:, w * F:(w + 1) * F], axis=AX.X, op=ALU.add,
                                        apply_absolute_value=True).then_inc(wsum_ready, 1)
            dve.wait_ge(small_ld, 16 * 5)
            dve.wait_ge(total_ready, 1)
            nc.vector.tensor_scalar(scale[:], ps[:, 7, 0:3], 1.0 / (2 * F * OD), None, ALU.mult).then_inc(total_read, 1)
            dve.wait_ge(total_read, 1)
            nc.vector.tensor_scalar(thr[:], scale[:], 0.5, None, ALU.mult).then_inc(schain, 1)
            nc.vector.tensor_scalar(nthr[:], scale[:], -0.5, None, ALU.mult).then_inc(schain, 1)
            nc.vector.tensor_scalar(gscale[:], scale[:, 0:1], 1.0 / XS, None, ALU.mult).then_inc(schain, 1)
            nc.vector.tensor_scalar(fprod[:], scale[:, 0:1], scale[:, 1:2], 1.0 / HS, ALU.mult, ALU.mult).then_inc(schain, 1)
            dve.wait_ge(schain, 4)
            nc.vector.tensor_scalar(fscale[:], fprod[:], scale[:, 2:3], None, ALU.mult).then_inc(scales_ready, 1)
            q_full(0)
            negatives(0)
            ternary(0)
            q_full(1)
            for c in range(DC):
                expand(c, 0, mg)
            q_full(2)
            negatives(1)
            ternary(1)
            expand(0, 0, mu)
            q_full(3)
            v_parts(0)
            x_low(0)
            expand(1, 0, mu)
            q_full(4)
            expand(2, 0, mu)
            expand(3, 0, mu)
            q_full(5)
            v_parts(1)
            q_full(6)
            x_low(1)
            q_full(7)
            def hidden(m, b, rows, first=False):
                n = 2 * m + b
                if first:
                    for ready in (qr_ready, q2_ready, q3_ready):
                        dve.wait_ge(ready, (B * DC - 1) + b)
                dve.wait_ge(sig_ready, n + 1)
                nc.vector.scalar_tensor_tensor(out=gated[0:rows, b, :], in0=ps[0:rows, 2 * b, :], scalar=HS / (XS * XS),
                                               in1=sig[0:rows, b, :], op0=ALU.mult, op1=ALU.mult).then_inc(gated_ready, 1)
                dve.wait_ge(gated_ready, n + 1)
                dve.wait_ge(up_ready, n + 1)
                if not first:
                    dve.wait_ge(hlo_ready, n - 1)
                nc.vector.tensor_tensor(hid[0:rows, b, :], ps[0:rows, 2 * b + 1, :], gated[0:rows, b, :],
                                        ALU.mult).then_inc(hid_ready, 1)

            hidden(0, 0, P, first=True)
            negatives(2)
            hidden(0, 1, P, first=True)
            ternary(2)
            for c in range(DC):
                hidden(1 + c // 2, c % 2, P)
                expand(c, 1, md)
            with dve.Fori(3, MF - 1) as m:
                for b in range(B):
                    hidden(m, b, P)
            for b in range(B):
                hidden(MF - 1, b, FL)

            for m in range(1, MF, 2):
                dve.wait_ge(mdt_ready, m + 1)
                nc.vector.tensor_copy(mdT[:, m, :], ps[:, 4 + m % 4, 0:D // 2].bitcast(FP16)).then_inc(mdT_ready[1], 1)

            dve.wait_ge(xb_ready, NT)

            def add_down(i, o, what):
                if "D" in what:
                    tile, row = o + 1, x_sb[:, o + 1, :]
                elif "d" in what and o == 1:
                    tile, row = i + 2, x_sb[:, bass.ds(i + 2, 1), :].squeeze(1)
                else:
                    return
                dve.wait_ge(down_ready, tile + 1)
                nc.vector.scalar_tensor_tensor(out=row, in0=ps[:, DOWN_BANK, :], scalar=fscale[:, 0:1], in1=row,
                                               op0=ALU.mult, op1=ALU.add).then_inc(down_used, 1)

            def add_output(t):
                dve.wait_ge(o_ready, t + 1)
                nc.vector.tensor_tensor(x_sb[:, t, :], ps[:, 2 + t % 2, :], x_sb[:, t, :], ALU.add).then_inc(y_ready, 1)

            def combine(i, o, u):
                g, t = group(i, o), slice(2 * u, 2 * u + 2)
                dve.wait_ge(sums_ready[u], g + 1)
                sums = ps[:, 6, :].rearrange("p (s e) -> p s e", e=SW)
                nc.vector.reciprocal(rden[:, t].rearrange("p t h -> p (t h)"), sums[:, :, 0]).then_inc(rden_ready, 1)
                nc.vector.tensor_reduce(osum[:, t].rearrange("p t h d -> p (t h) d"),
                                        sums[:, :, 1:VW].rearrange("p s (r d) -> p s d r", r=3),
                                        axis=AX.X, op=ALU.add).then_inc(osum_ready[u], 1)

            def attention(i, o, u):
                g, t = group(i, o), slice(2 * u, 2 * u + 2)
                dve.wait_ge(osum_ready[u], g + 1)
                dst = attn[:, bass.ds(i + o // 2, 1), t, o % 2 * GH * HD:(o % 2 + 1) * GH * HD].squeeze(1)
                nc.vector.tensor_tensor(dst.rearrange("p t (h d) -> p t h d", h=GH), osum[:, t],
                                        rden[:, t].unsqueeze(3).to_broadcast([P, 2, GH, HD]), ALU.mult).then_inc(normed[u], 1)

            def step(i, o, what):
                def maxima(n):
                    if "m" not in what:
                        return
                    g, par = group(i, o + 3), (o + 3) % 2
                    t, heads, per = UNITS[n]
                    keys = (t + 1) * P
                    banks = slice(2 * (n % 2), 2 * (n % 2) + len(heads) // per)
                    dve.wait_ge(rows_ready, NU * g + n + 1)
                    if t < 2:
                        src = ps[:, banks, 0:per * keys].rearrange("p b (h k) -> p (b h) k", h=per)
                    else:
                        src = ps[:, banks, 0:keys]
                    nc.vector.tensor_reduce(negm[:, par, heads[0]:heads[-1] + 1, t], src, axis=AX.X, op=ALU.max,
                                            negate=True).then_inc(rows_used, 1)

                def low(n):
                    if "e" not in what:
                        return
                    e, par, s = group(i, o + 1), (o + 1) % 2, LOW_DVE[n]
                    dve.wait_ge(high_ready, NBLK * e + s + 1)
                    nc.vector.tensor_tensor(probs[par][1][:, s, :], full[:, s % HELD, :], probs[par][0][:, s, :],
                                            ALU.subtract).then_inc(low_ready, 1)

                def columns():
                    if "r" not in what:
                        return
                    g, par = group(i, o + 2), o % 2
                    dve.wait_ge(mt_ready, g + 1)
                    if "s" in what:
                        dve.wait_ge(mrow_st[par], 16 * (i + o // 2 + 1))
                    nc.vector.tensor_copy(mrows[:, par, :], ps[0:2 * GH * TT, MAXIMA_BANK, 0:P // 2].bitcast(BF16)).then_inc(mt_read, 1)

                for n in range(NU):
                    maxima(n)
                    if n == 0 and "p" in what:
                        combine(i, o - 1, 0)
                        attention(i, o - 1, 0)
                    if n == COPIED_AFTER:
                        columns()
                    if n in LOW_AFTER:
                        low(LOW_AFTER.index(n))
                    if n == 3 and "s" in what:
                        combine(i, o, 1)
                        attention(i, o, 1)
                    if "o" in what and n in ADDED_AT[o]:
                        add_output(ADDED_AT[o][n])
                add_down(i, o, what)
                if "m" in what:
                    g, par = group(i, o + 3), (o + 3) % 2
                    dve.wait_ge(rows_used, NU * (g + 1))
                    if "e" in what:
                        dve.wait_ge(mt_ready, g - 1)
                    flat, shift = negm[:, par].rearrange("p h t -> p (h t)"), float(np.log(PS)) * HD ** 0.5
                    nc.vector.tensor_scalar(mparts[:, par, 0, :], flat, shift, None, ALU.add).then_inc(m1_ready, 1)
                    dve.wait_ge(m1_ready, g + 1)
                    nc.vector.scalar_tensor_tensor(out=mparts[:, par, 1, :], in0=flat, scalar=shift, in1=mparts[:, par, 0, :],
                                                   op0=ALU.add, op1=ALU.subtract).then_inc(mparts_ready, 1)

            for st in STEPS:
                if st == "loop":
                    with dve.Fori(*LOOPED) as i:
                        for o in range(2):
                            step(i, o, "mreswpd")
                else:
                    step(*st)
            combine(*STEPS[-1][0:2], 0)
            attention(*STEPS[-1][0:2], 0)

            for t in range(TT, NT):
                add_output(t)

        @block.tensor
        def _(pe):
            pe.wait_ge(zeros_ready, 1)
            for _ in range(WARM_UPS):
                nc.tensor.matmul(ps[:, 7, :], zeros[:, 0:P], zeros, start=True, stop=True)
            pe.wait_ge(consts, 5)

            def transposes(n):
                pe.wait_ge(xn_ready, n + 1)
                if n >= 2:
                    pe.wait_ge(xnT_ready, n - 1)
                for c in range(DC):
                    last = nc.tensor.transpose(ps[:, n % 2, c * P:(c + 1) * P], xn[:, n % TT, c * P:(c + 1) * P], identf[:])
                last.then_inc(xt_ready, 1)

            def project_q(u):
                b, m = u // DC, u % DC
                if b:
                    pe.wait_ge(q1_ready, m + 1)
                    pe.wait_ge(qf_ready, m + 1)
                for c in range(DC):
                    last = nc.tensor.matmul(ps[:, 2 + m, :], wq_sb[:, c, m * P:(m + 1) * P], xnT[:, c, b * T:(b + 1) * T],
                                            start=c == 0, stop=c == DC - 1)
                last.then_inc(q_ready, 1)

            def project_kv(b):
                if b:
                    pe.wait_ge(kf_ready, b)
                for c in range(DC):
                    last = nc.tensor.matmul(ps[0:KV, 6, :], wkv_sb[:, c, :], xnT[:, c, b * T:(b + 1) * T],
                                            start=c == 0, stop=c == DC - 1)
                last.then_inc(k_ready, 1)

            def transpose_v(b):
                pe.wait_ge(kf_ready, b + 1)
                if b:
                    pe.wait_ge(vsb_ready, b)
                else:
                    pe.wait_ge(total_read, 1)
                for i in range(TT):
                    last = nc.tensor.transpose(ps[:, 7, i * HD:(i + 1) * HD], kvf[BANDS:KV, i * P:(i + 1) * P],
                                               identf[BANDS:KV, BANDS:KV])
                last.then_inc(v_ready, 1)

            for n in range(TT):
                transposes(n)
            pe.wait_ge(xnT_ready, TT)
            pe.wait_ge(wq_ld, 16)
            project_q(0)
            for n in range(TT, NT):
                transposes(n)
            project_q(1)
            pe.wait_ge(wsum_ready, 3)
            nc.tensor.matmul(ps[:, 7, 0:3], ones[:], wsum[:], start=True, stop=True).then_inc(total_ready, 1)
            pe.wait_ge(wkv_ld, 16)
            project_kv(0)
            project_q(2)
            transpose_v(0)
            project_q(3)
            pe.wait_ge(xnT_ready, NT)
            project_kv(1)
            project_q(4)
            project_q(5)
            transpose_v(1)
            for u in range(6, B * DC):
                project_q(u)


            def hidden(m, b, rows, first=False):
                n = 2 * m + b
                t = slice(b * T, (b + 1) * T)
                if first:
                    pe.wait_ge(xlo_ready, b + 1)
                    pe.wait_ge(q1_ready, DC + 2 * b)
                    pe.wait_ge(qf_ready, DC + 2 * b)
                else:
                    pe.wait_ge(hid_ready, n - 1)
                for w, bank, ready in ((mg, 2 * b, gate_ready), (mu, 2 * b + 1, up_ready)):
                    if first:
                        pe.wait_ge(built, DC * (bank % 2 + 1))
                    for c in range(DC):
                        for h, xh in enumerate((xhi, xlo)):
                            last = nc.tensor.matmul(ps[0:rows, bank, :], w[:, c, bass.ds(m * P, rows)], xh[:, c, t],
                                                    start=c == 0 and h == 0, stop=c == DC - 1 and h == 1)
                    last.then_inc(ready, 1)

            for b in range(B):
                hidden(0, b, P, first=True)
            with pe.Fori(1, MF - 1) as m:
                for b in range(B):
                    hidden(m, b, P)
            for b in range(B):
                hidden(MF - 1, b, FL)

            pe.wait_ge(built, DC * 3)
            pe.wait_ge(q1_ready, B * DC)
            pe.wait_ge(qf_ready, B * DC)
            pe.wait_ge(kf_ready, B)
            pe.wait_ge(vsb_ready, B)
            for m in range(MF):
                rows = P if m < MF - 1 else FL
                if m >= 4:
                    pe.wait_ge(mdT_ready[m % 2], (m - 4) // 2 + 1)
                for c in range(DC):
                    last = nc.tensor.transpose(ps[0:rows, 4 + m % 4, c * P // 2:(c + 1) * P // 2].bitcast(FP16),
                                               md[:, c, m * P:m * P + rows], ident16[:])
                last.then_inc(mdt_ready, 1)

            pe.wait_ge(hid_ready, 2 * MF)

            def down(i, o, what, s):
                if "D" in what:
                    tile, pieces = o + 1, DOWN_WHOLE
                elif "d" in what:
                    tile, pieces = i + 2, DOWN_HALF[o]
                else:
                    return
                if s not in pieces:
                    return
                first, end = pieces[s]
                if first == 0 and ("d" in what or tile):
                    pe.wait_ge(down_used, tile)
                elif first == 0:
                    pe.wait_ge(mdT_ready[0], -(-MF // 2))
                    pe.wait_ge(mdT_ready[1], MF // 2)
                    pe.wait_ge(hlo_ready, 2 * MF)
                    pe.wait_ge(hhi_ready, 2 * MF)
                cols = slice(tile * P, (tile + 1) * P) if "D" in what else bass.ds(tile * P, P)
                for m in range(first, end):
                    rows = P if m < MF - 1 else FL
                    for h in range(2):
                        last = nc.tensor.matmul(ps[:, DOWN_BANK, :], hbuf[0:rows, h, m, cols], mdT[0:rows, m, :],
                                                start=m == 0 and h == 0, stop=m == MF - 1 and h == 1, skip_group_check=True)
                if end == MF:
                    last.then_inc(down_ready, 1)

            pe.wait_ge(kstack_ready, B)

            def attention_transposes(t):
                if t >= 2:
                    pe.wait_ge(attnT_ready, t - 1)
                for c in range(DC):
                    last = nc.tensor.transpose(ps[:, t % 2, c * P:(c + 1) * P], attn[:, t // TT * DC + c, t % TT, :], identf[:])
                last.then_inc(at_ready, 1)

            def project_out(t, chunks=range(DC)):
                if chunks[0] == 0:
                    pe.wait_ge(attnT_ready, t + 1)
                    if t >= 2:
                        pe.wait_ge(y_ready, t - 1)
                for c in chunks:
                    last = nc.tensor.matmul(ps[:, 2 + t % 2, :], attnT[:, t % 2, c, :], wo_sb[:, c, :],
                                            start=c == 0, stop=c == DC - 1, skip_group_check=True)
                if chunks[-1] == DC - 1:
                    last.then_inc(o_ready, 1)

            def step(i, o, what):
                for s, (kc, t) in enumerate(BLOCKS):
                    down(i, o, what, s)
                    if "o" in what and s in TRANSPOSED_AT[o]:
                        tile = TRANSPOSED_AT[o][s]
                        if tile == 0:
                            pe.wait_ge(rows_used, NU * NG)
                            pe.wait_ge(normed[0], GB)
                            pe.wait_ge(normed[1], GB)
                        attention_transposes(tile)
                    for tile, c in OUT_AT[o].get(s, []) if "o" in what else []:
                        if tile == 0 and c == 0:
                            pe.wait_ge(wo_ld, 16)
                        if tile == 1 and c == 0:
                            pe.wait_ge(mt_read, NG)
                        project_out(tile, [c])
                    if "m" in what and s in UNIT_AT:
                        g, n = group(i, o + 3), UNIT_AT[s]
                        if s == 0:
                            pe.wait_ge(stack_ld[(o + 3) % 2], 16 * len(PAIRS) * (i + (o + 3) // 2 + 1))
                        if "r" in what or n >= 2:
                            pe.wait_ge(rows_used, NU * g + n - 1)
                        if "r" in what and n == 3:
                            pe.wait_ge(mt_read, g)
                        ut, heads, per = UNITS[n]
                        keys = (ut + 1) * P
                        for at in range(len(heads) // per):
                            bank = 2 * (n % 2) + at
                            diag = ps[:, bank, 0:per * keys].rearrange("p (h k) -> p h k", h=per)[:, :, keys - P:keys]
                            nc.tensor.matmul(diag, identb[:], maskq[:].unsqueeze(1).to_broadcast([P, per, P]),
                                             start=True, stop=False, skip_group_check=True)
                            for a in range(per):
                                h = heads[at * per + a]
                                last = nc.tensor.matmul(
                                    ps[:, bank, a * keys:(a + 1) * keys],
                                    qstack[0:BANDS, bass.ds((g % SLOTS) * GW + h * T + ut * P, P)],
                                    kstack[0:BANDS, bass.ds((g // GB) * T, keys)],
                                    start=False, stop=a == per - 1, skip_group_check=True)
                        last.then_inc(rows_ready, 1)
                    if "r" in what and s == MAXIMA_AT:
                        g, par = group(i, o + 2), o % 2
                        pe.wait_ge(mparts_ready, g + 1)
                        if "m" not in what:
                            pe.wait_ge(rows_used, NU * NG)
                        nc.tensor.transpose(ps[0:2 * GH * TT, MAXIMA_BANK, 0:P // 2].bitcast(BF16),
                                            mparts[:, par].rearrange("p a s -> p (a s)"), identb[:]).then_inc(mt_ready, 1)
                    if "e" in what:
                        g = group(i, o + 1)
                        if s == 0:
                            pe.wait_ge(mrow_ld[(o + 1) % 2], 16 * (i + (o + 1) // 2 + 1))
                        if "s" in what or s >= 2:
                            pe.wait_ge(exp_ready, NBLK * g + s - 1)
                        qs = qstack[:, bass.ds((g % SLOTS) * GW, GW)].rearrange("r (h q) -> r h q", h=GH)
                        cols = ps[:, 4 + s % 2, :].rearrange("p (h q) -> p h q", h=GH)
                        if kc == t:
                            nc.tensor.matmul(cols, identb[:], maskk[:].unsqueeze(1).to_broadcast([P, GH, P]),
                                             start=True, stop=False)
                        nc.tensor.matmul(cols, kstack[:, bass.ds((g // GB) * T + kc * P, P)], qs[:, :, t * P:(t + 1) * P],
                                         start=kc != t, stop=True).then_inc(cols_ready, 1)
                    if "s" in what:
                        g, par = group(i, o), o % 2
                        if s == FIRST_SUMS and "w" in what:
                            pe.wait_ge(normed[0], g)
                        for bound, upto in ((FIRST_SUMS, LAST_BLOCK[2]), (FIRST_TILE_3, NBLK - 1)):
                            if s == bound:
                                pe.wait_ge(low_ready, len(LOW_DVE) * g + sum(b <= upto for b in LOW_DVE))
                                pe.wait_ge(plow_ready, len(LOW_POOL) * g + sum(b <= upto for b in LOW_POOL))
                                pe.wait_ge(high_ready, NBLK * g + upto + 1)
                        if s == FIRST_LOW_TILES:
                            pe.wait_ge(normed[1], g + 1)
                        for qt, h in SUMS_AT[s]:
                            for kt in range(qt + 1):
                                for a, width in enumerate((VW, VL)):
                                    at = ((qt % 2) * GH + h) * SW
                                    last = nc.tensor.matmul(
                                        ps[:, 6, at:at + width],
                                        probs[par][a][:, BLOCKS.index((kt, qt)), h * P:(h + 1) * P],
                                        v_sb[:, bass.ds((g // GB) * TT + kt, 1), 0:width].squeeze(1),
                                        start=kt == 0 and a == 0, stop=kt == qt and a == 1, skip_group_check=True)
                            if (qt, h) in LAST_SUMS:
                                last.then_inc(sums_ready[qt // 2], 1)

            for st in STEPS:
                if st == "loop":
                    with pe.Fori(*LOOPED) as i:
                        for o in range(2):
                            step(i, o, "mreswpd")
                else:
                    step(*st)

            pe.wait_ge(normed[0], NG)
            pe.wait_ge(normed[1], NG)
            attention_transposes(TT)
            for t in range(TT, NT):
                if t + 1 < NT:
                    attention_transposes(t + 1)
                project_out(t)


def octonion_signs():
    s = np.zeros((J, J, J), np.float32)
    s[0, 0, 0] = 1.0
    for i in range(1, J):
        s[0, i, i] = s[i, 0, i] = 1.0
        s[i, i, 0] = -1.0
    for a, b, c in [(1, 2, 3), (1, 4, 5), (1, 7, 6), (2, 4, 6), (2, 5, 7), (3, 4, 7), (3, 6, 5)]:
        for p, q, r in ((a, b, c), (b, c, a), (c, a, b)):
            s[p, q, r], s[q, p, r] = 1.0, -1.0
    return s


def slots(w, component_last):
    w = w.transpose(0, 2, 1) if component_last else w
    halves = [w[[j ^ h for j in range(J)]].transpose(1, 0, 2).reshape(OD, F) for h in range(2)]
    return np.ascontiguousarray(np.concatenate(halves, 0))


def kernel(**inputs):
    import concourse.bacc as bacc
    from concourse.bass_utils import run_bass_kernel_spmd

    a = {k.replace("L0_", ""): np.asarray(v) for k, v in inputs.items()}
    s = octonion_signs()
    signs = np.zeros((P, 2, DC, J), np.float32)
    for c in range(DC):
        for h in range(2):
            for k in range(J):
                rows = slice(h * OD, (h + 1) * OD)
                i = 2 * c + h
                signs[rows, 0, c, k] = s[i ^ k, i, k]
                signs[rows, 1, c, k] = s[i ^ k, k, i]
    bands = np.zeros((BANDS, 3), np.float32)
    for r, (_, part) in enumerate(PAIRS):
        bands[r * HD:(r + 1) * HD, part] = 1.0
    arrays = {
        "x": a["attn_x"].reshape(TOK, D),
        "wqT": a["attn_wq_w"].T,
        "wkvT": np.concatenate([a["attn_wk_w"].T] * len(PAIRS) + [a["attn_wv_w"].T], 1),
        "woT": a["attn_wo_w"].T,
        "bq": a["attn_wq_b"].reshape(DC, P).T,
        "bkv": np.concatenate([a["attn_wk_b"]] * len(PAIRS) + [a["attn_wv_b"]]).reshape(KV, 1),
        "bo": a["attn_wo_b"],
        "wg": slots(a["ffn_w_gate"], True),
        "wu": slots(a["ffn_w_up"], True),
        "wd": slots(a["ffn_w_down"], False),
        "signs": signs.reshape(P, 2 * DC * J),
        "bands": bands,
    }
    arrays = {k: np.ascontiguousarray(v) for k, v in arrays.items()}
    nc = bacc.Bacc("TRN2", target_bir_lowering=False, num_devices=1)
    args = [nc.dram_tensor(k, v.shape, mybir.dt.from_np(v.dtype), kind="ExternalInput").ap() for k, v in arrays.items()]
    out = nc.dram_tensor("out", (TOK, D), FP32, kind="ExternalOutput").ap()
    build(nc, *args, out)
    r = run_bass_kernel_spmd(nc, [arrays], core_ids=[0])
    return r.results[0]["out"].reshape(a["attn_x"].shape)
```
